# Optimizing a Trainium2 kernel written in Bass

```python
import numpy as np
import jax
import jax.numpy as jnp

def _softmax(x, axis=-1):
    return jax.nn.softmax(x, axis=axis)

def _gelu(x):
    return jax.nn.gelu(x, approximate=True)

def _silu(x):
    return jax.nn.silu(x)

def _sigmoid(x):
    return jax.nn.sigmoid(x)

def _layernorm(x, axis=-1, eps=1e-05):
    m = jnp.mean(x, axis=axis, keepdims=True)
    v = jnp.var(x, axis=axis, keepdims=True)
    return (x - m) / jnp.sqrt(v + eps)

def _scatter_add(tgt, idx, src, axis=0):
    return tgt.at[idx].add(src)

def _segment_sum(src, seg, n):
    return jax.ops.segment_sum(src, seg, n)
kernel_name = 'mk_flamingo_gated_d2_seqx_r4_9d2ee8'

def setup_inputs(seed: int=0):
    np.random.seed(seed)
    _w = jnp.asarray

    def _rec_inputs():
        import jax
        import jax.numpy as jnp
        _rk = jax.random.key(seed)
        x = -0.0003542 + 1 * jax.random.normal(jax.random.fold_in(_rk, 1), (4, 512, 256), jnp.float32)
        _lenS = 512 - jax.random.randint(jax.random.fold_in(_rk, 7), (4,), 0, max(1, 512 // 4) + 1, jnp.int32)
        _lenS2 = 512 - jax.random.randint(jax.random.fold_in(_rk, 8), (4,), 0, max(1, 512 // 4) + 1, jnp.int32)
        _ctx_1024P = jax.random.normal(jax.random.fold_in(_rk, 11), (4, 16, 256), jnp.float32)
        _ctx_1024c = jax.random.dirichlet(jax.random.fold_in(_rk, 511), 0.3 * jnp.ones((16,), jnp.float32), (4, 512))
        _ctx_1024t = jnp.einsum('bsk,bkd->bsd', _ctx_1024c, _ctx_1024P)
        _ctx_1024t = _ctx_1024t * jax.lax.rsqrt(jnp.mean(jnp.square(_ctx_1024t)) + 1e-12) * 0.953939
        ctx_1024 = -4.4511e-05 + 0.999885 * (_ctx_1024t + 0.3 * jax.random.normal(jax.random.fold_in(_rk, 611), (4, 512, 256), jnp.float32))
        _g = jax.random.normal(jax.random.fold_in(_rk, 9001), (2, 2), jnp.float32)
        _g = jnp.sign(_g) * jnp.maximum(jnp.abs(_g), 1.0) + (_g == 0) * 1.0
        g_xattn = _g[0]
        g_ffn = _g[1]
        return (x, ctx_1024, g_xattn, g_ffn)
    x, ctx_1024, g_xattn, g_ffn = _rec_inputs()

    def _L0_xattn_setup():
        import jax, jax.numpy as jnp
        import numpy as np
        D_MODEL = 256
        NUM_HEADS = 16
        MAX_LEN = 125
        D_K = D_MODEL // NUM_HEADS
        key = jax.random.key(seed)
        ks = jax.random.split(key, 10)
        B, L = (8, 125)
        s = 1.0 / np.sqrt(D_MODEL)
        return {'query': jax.random.normal(ks[0], (B, L, D_MODEL), dtype=jnp.float32), 'key': jax.random.normal(ks[1], (B, L, D_MODEL), dtype=jnp.float32), 'value': jax.random.normal(ks[2], (B, L, D_MODEL), dtype=jnp.float32), 'Wq': jax.random.normal(ks[3], (D_MODEL, D_MODEL), dtype=jnp.float32) * s, 'bq': jnp.zeros((D_MODEL,), dtype=jnp.float32), 'Wk': jax.random.normal(ks[4], (D_MODEL, D_MODEL), dtype=jnp.float32) * s, 'bk': jnp.zeros((D_MODEL,), dtype=jnp.float32), 'Wv': jax.random.normal(ks[5], (D_MODEL, D_MODEL), dtype=jnp.float32) * s, 'bv': jnp.zeros((D_MODEL,), dtype=jnp.float32), 'rel_emb': jax.random.normal(ks[6], (NUM_HEADS, 2 * MAX_LEN - 1), dtype=jnp.float32)}
    _L0_xattn_all = _L0_xattn_setup()
    _L0_xattn_in = {k: v for k, v in _L0_xattn_all.items() if k in ('Wq', 'bq', 'Wk', 'bk', 'Wv', 'bv', 'rel_emb')}
    del _L0_xattn_all

    def _L0_ffn_setup():
        import jax, jax.numpy as jnp
        import numpy as np
        B, S, D_MODEL, D_FF = (4, 512, 256, 1024)

        def _quantum_transform(hidden, theta, w_real, w_imag):
            imag = w_imag * jnp.sin(theta + hidden * 0.1)
            quantum_phase = jnp.cos(theta) * w_real + jnp.sin(theta) * w_imag
            return hidden + quantum_phase * imag * 0.1
        key = jax.random.key(seed)
        ks = jax.random.split(key, 8)
        return {'x': jax.random.normal(ks[0], (B, S, D_MODEL), dtype=jnp.float32), 'W1': jax.random.normal(ks[1], (D_MODEL, D_FF), dtype=jnp.float32) * (1.0 / np.sqrt(D_MODEL)), 'b1': jnp.zeros((D_FF,), dtype=jnp.float32), 'quantum_phases': jax.random.normal(ks[2], (D_FF,), dtype=jnp.float32) * (2.0 * np.pi), 'quantum_weights_real': jax.random.normal(ks[3], (D_FF,), dtype=jnp.float32) * 0.1, 'quantum_weights_imag': jax.random.normal(ks[4], (D_FF,), dtype=jnp.float32) * 0.1, 'W2': jax.random.normal(ks[5], (D_FF, D_MODEL), dtype=jnp.float32) * (1.0 / np.sqrt(D_FF)), 'b2': jnp.zeros((D_MODEL,), dtype=jnp.float32)}
    _L0_ffn_all = _L0_ffn_setup()
    _L0_ffn_in = {k: v for k, v in _L0_ffn_all.items() if k in ('W1', 'b1', 'quantum_phases', 'quantum_weights_real', 'quantum_weights_imag', 'W2', 'b2')}
    del _L0_ffn_all

    def _L1_xattn_setup():
        import jax, jax.numpy as jnp
        import numpy as np
        D_MODEL = 256
        NUM_HEADS = 16
        HEAD_DIM = D_MODEL // NUM_HEADS
        key = jax.random.key(seed)
        ks = jax.random.split(key, 10)
        B, SQ, SKV = (4, 512, 512)
        s = 1.0 / np.sqrt(D_MODEL)
        return {'query': jax.random.normal(ks[0], (B, SQ, D_MODEL), jnp.float32), 'key_value': jax.random.normal(ks[1], (B, SKV, D_MODEL), jnp.float32), 'Wq': jax.random.normal(ks[2], (D_MODEL, D_MODEL), jnp.float32) * s, 'bq': jnp.zeros((D_MODEL,), jnp.float32), 'Wk': jax.random.normal(ks[3], (D_MODEL, D_MODEL), jnp.float32) * s, 'bk': jnp.zeros((D_MODEL,), jnp.float32), 'Wv': jax.random.normal(ks[4], (D_MODEL, D_MODEL), jnp.float32) * s, 'bv': jnp.zeros((D_MODEL,), jnp.float32), 'Wo': jax.random.normal(ks[5], (D_MODEL, D_MODEL), jnp.float32) * s, 'bo': jnp.zeros((D_MODEL,), jnp.float32)}
    _L1_xattn_all = _L1_xattn_setup()
    _L1_xattn_in = {k: v for k, v in _L1_xattn_all.items() if k in ('Wq', 'bq', 'Wk', 'bk', 'Wv', 'bv', 'Wo', 'bo')}
    del _L1_xattn_all

    def _L1_ffn_setup():
        import jax, jax.numpy as jnp
        import numpy as np
        LN_EPS = 1e-05
        NORM_EPS = 1e-12

        def _layernorm(x, gamma, beta):
            mu = x.mean(axis=-1, keepdims=True)
            var = ((x - mu) ** 2).mean(axis=-1, keepdims=True)
            return (x - mu) * jax.lax.rsqrt(var + LN_EPS) * gamma + beta

        def _l2norm(x, axis):
            n = jnp.sqrt((x ** 2).sum(axis=axis, keepdims=True))
            return x / jnp.maximum(n, NORM_EPS)
        key = jax.random.key(seed)
        ks = jax.random.split(key, 4)
        B, N, D, E, S, H = (64, 64, 256, 16, 16, 64)
        x = jax.random.normal(ks[0], (B, N, D), dtype=jnp.float32)
        mu = jax.random.normal(ks[1], (D, E, S), dtype=jnp.float32) / np.sqrt(D)
        w1 = jax.random.normal(ks[2], (E, D, H), dtype=jnp.float32) * np.sqrt(2.0 / D)
        w2 = jax.random.normal(ks[3], (E, H, D), dtype=jnp.float32) * np.sqrt(2.0 / (H + D))
        return {'x': x, 'ln_gamma': jnp.ones((D,), jnp.float32), 'ln_beta': jnp.zeros((D,), jnp.float32), 'mu': mu, 'scale': jnp.ones((1,), jnp.float32), 'w1': w1, 'b1': jnp.zeros((E, H), jnp.float32), 'w2': w2, 'b2': jnp.zeros((E, D), jnp.float32)}
    _L1_ffn_all = _L1_ffn_setup()
    _L1_ffn_in = {k: v for k, v in _L1_ffn_all.items() if k in ('ln_gamma', 'ln_beta', 'mu', 'scale', 'w1', 'b1', 'w2', 'b2')}
    del _L1_ffn_all
    return {'x': x, 'ctx_1024': ctx_1024, 'g_xattn': g_xattn, 'g_ffn': g_ffn, 'L0_xattn_Wq': _L0_xattn_in['Wq'], 'L0_xattn_bq': _L0_xattn_in['bq'], 'L0_xattn_Wk': _L0_xattn_in['Wk'], 'L0_xattn_bk': _L0_xattn_in['bk'], 'L0_xattn_Wv': _L0_xattn_in['Wv'], 'L0_xattn_bv': _L0_xattn_in['bv'], 'L0_xattn_rel_emb': _L0_xattn_in['rel_emb'], 'L0_ffn_W1': _L0_ffn_in['W1'], 'L0_ffn_b1': _L0_ffn_in['b1'], 'L0_ffn_quantum_phases': _L0_ffn_in['quantum_phases'], 'L0_ffn_quantum_weights_real': _L0_ffn_in['quantum_weights_real'], 'L0_ffn_quantum_weights_imag': _L0_ffn_in['quantum_weights_imag'], 'L0_ffn_W2': _L0_ffn_in['W2'], 'L0_ffn_b2': _L0_ffn_in['b2'], 'L1_xattn_Wq': _L1_xattn_in['Wq'], 'L1_xattn_bq': _L1_xattn_in['bq'], 'L1_xattn_Wk': _L1_xattn_in['Wk'], 'L1_xattn_bk': _L1_xattn_in['bk'], 'L1_xattn_Wv': _L1_xattn_in['Wv'], 'L1_xattn_bv': _L1_xattn_in['bv'], 'L1_xattn_Wo': _L1_xattn_in['Wo'], 'L1_xattn_bo': _L1_xattn_in['bo'], 'L1_ffn_ln_gamma': _L1_ffn_in['ln_gamma'], 'L1_ffn_ln_beta': _L1_ffn_in['ln_beta'], 'L1_ffn_mu': _L1_ffn_in['mu'], 'L1_ffn_scale': _L1_ffn_in['scale'], 'L1_ffn_w1': _L1_ffn_in['w1'], 'L1_ffn_b1': _L1_ffn_in['b1'], 'L1_ffn_w2': _L1_ffn_in['w2'], 'L1_ffn_b2': _L1_ffn_in['b2']}

def reference(x, ctx_1024, g_xattn, g_ffn, L0_xattn_Wq, L0_xattn_bq, L0_xattn_Wk, L0_xattn_bk, L0_xattn_Wv, L0_xattn_bv, L0_xattn_rel_emb, L0_ffn_W1, L0_ffn_b1, L0_ffn_quantum_phases, L0_ffn_quantum_weights_real, L0_ffn_quantum_weights_imag, L0_ffn_W2, L0_ffn_b2, L1_xattn_Wq, L1_xattn_bq, L1_xattn_Wk, L1_xattn_bk, L1_xattn_Wv, L1_xattn_bv, L1_xattn_Wo, L1_xattn_bo, L1_ffn_ln_gamma, L1_ffn_ln_beta, L1_ffn_mu, L1_ffn_scale, L1_ffn_w1, L1_ffn_b1, L1_ffn_w2, L1_ffn_b2):
    import jax
    import jax.numpy as jnp

    def _L0_xattn_ref(query, key, value, Wq, bq, Wk, bk, Wv, bv, rel_emb):
        import jax, jax.numpy as jnp
        import numpy as np
        D_MODEL = 256
        NUM_HEADS = 16
        MAX_LEN = 125
        D_K = D_MODEL // NUM_HEADS
        B, Lq, _ = query.shape
        Lk = key.shape[1]
        H, dk = (NUM_HEADS, D_K)
        q = (query @ Wq + bq).reshape(B, Lq, H, dk).transpose(0, 2, 1, 3)
        k = (key @ Wk + bk).reshape(B, Lk, H, dk).transpose(0, 2, 1, 3)
        v = (value @ Wv + bv).reshape(B, Lk, H, dk).transpose(0, 2, 1, 3)
        scores = jnp.einsum('bhqd,bhkd->bhqk', q, k) / jnp.sqrt(jnp.float32(dk))
        rel_idx = jnp.arange(Lq)[:, None] - jnp.arange(Lk)[None, :] + MAX_LEN - 1
        bias = rel_emb[:, rel_idx]
        scores = scores + bias[None]
        attn = jax.nn.softmax(scores, axis=-1)
        out = jnp.einsum('bhqk,bhkd->bhqd', attn, v)
        return out.transpose(0, 2, 1, 3).reshape(B, Lq, H * dk)

    def _L0_ffn_ref(x, W1, b1, quantum_phases, quantum_weights_real, quantum_weights_imag, W2, b2):
        import jax, jax.numpy as jnp
        import numpy as np
        B, S, D_MODEL, D_FF = (4, 512, 256, 1024)

        def _quantum_transform(hidden, theta, w_real, w_imag):
            imag = w_imag * jnp.sin(theta + hidden * 0.1)
            quantum_phase = jnp.cos(theta) * w_real + jnp.sin(theta) * w_imag
            return hidden + quantum_phase * imag * 0.1
        hidden = jnp.einsum('bsd,df->bsf', x, W1) + b1
        q = _quantum_transform(hidden, quantum_phases, quantum_weights_real, quantum_weights_imag)
        act = jax.nn.relu(q)
        return jnp.einsum('bsf,fd->bsd', act, W2) + b2

    def _L1_xattn_ref(query, key_value, Wq, bq, Wk, bk, Wv, bv, Wo, bo):
        import jax, jax.numpy as jnp
        import numpy as np
        D_MODEL = 256
        NUM_HEADS = 16
        HEAD_DIM = D_MODEL // NUM_HEADS
        B, SQ, _ = query.shape
        SKV = key_value.shape[1]
        H, Dh = (NUM_HEADS, HEAD_DIM)
        Q = (query @ Wq.T + bq).reshape(B, SQ, H, Dh).transpose(0, 2, 1, 3)
        K = (key_value @ Wk.T + bk).reshape(B, SKV, H, Dh).transpose(0, 2, 1, 3)
        V = (key_value @ Wv.T + bv).reshape(B, SKV, H, Dh).transpose(0, 2, 1, 3)
        scale = jnp.asarray(np.sqrt(Dh), query.dtype)
        scores = jnp.einsum('bhqd,bhkd->bhqk', Q, K) / scale
        weights = jax.nn.softmax(scores, axis=-1)
        attn = jnp.einsum('bhqk,bhkd->bhqd', weights, V)
        attn = attn.transpose(0, 2, 1, 3).reshape(B, SQ, H * Dh)
        return attn @ Wo.T + bo

    def _L1_ffn_ref(x, ln_gamma, ln_beta, mu, scale, w1, b1, w2, b2):
        import jax, jax.numpy as jnp
        import numpy as np
        LN_EPS = 1e-05
        NORM_EPS = 1e-12

        def _layernorm(x, gamma, beta):
            mu = x.mean(axis=-1, keepdims=True)
            var = ((x - mu) ** 2).mean(axis=-1, keepdims=True)
            return (x - mu) * jax.lax.rsqrt(var + LN_EPS) * gamma + beta

        def _l2norm(x, axis):
            n = jnp.sqrt((x ** 2).sum(axis=axis, keepdims=True))
            return x / jnp.maximum(n, NORM_EPS)
        B, N, D = x.shape
        _, E, S = mu.shape
        xn = _layernorm(x, ln_gamma, ln_beta)
        x_unit = _l2norm(xn, axis=-1)
        mu_unit = _l2norm(mu, axis=0)
        logits = jnp.einsum('bnd,des->bnes', x_unit * scale, mu_unit)
        dispatch = jax.nn.softmax(logits, axis=1)
        combine = jax.nn.softmax(logits.reshape(B, N, E * S), axis=-1).reshape(B, N, E, S)
        slot_in = jnp.einsum('bnd,bnes->besd', xn, dispatch)
        h = jax.nn.gelu(jnp.einsum('besd,edh->besh', slot_in, w1) + b1[None, :, None, :], approximate=False)
        slot_out = jnp.einsum('besh,ehd->besd', h, w2) + b2[None, :, None, :]
        out = jnp.einsum('besd,bnes->bnd', slot_out, combine)
        return out
    x = x + jnp.tanh(g_xattn[0]) * _L0_xattn_ref(_layernorm(x, axis=-1), ctx_1024, ctx_1024, L0_xattn_Wq, L0_xattn_bq, L0_xattn_Wk, L0_xattn_bk, L0_xattn_Wv, L0_xattn_bv, L0_xattn_rel_emb)
    x = x + jnp.tanh(g_ffn[0]) * _L0_ffn_ref(_layernorm(x, axis=-1), L0_ffn_W1, L0_ffn_b1, L0_ffn_quantum_phases, L0_ffn_quantum_weights_real, L0_ffn_quantum_weights_imag, L0_ffn_W2, L0_ffn_b2)
    x = x + jnp.tanh(g_xattn[1]) * _L1_xattn_ref(_layernorm(x, axis=-1), ctx_1024, L1_xattn_Wq, L1_xattn_bq, L1_xattn_Wk, L1_xattn_bk, L1_xattn_Wv, L1_xattn_bv, L1_xattn_Wo, L1_xattn_bo)
    x = x + jnp.tanh(g_ffn[1]) * _L1_ffn_ref(_layernorm(x, axis=-1), L1_ffn_ln_gamma, L1_ffn_ln_beta, L1_ffn_mu, L1_ffn_scale, L1_ffn_w1, L1_ffn_b1, L1_ffn_w2, L1_ffn_b2)
    return x

_drawn_inputs = setup_inputs


def setup_inputs(seed=0):
    import zlib

    import numpy as np

    out = dict(_drawn_inputs(seed))
    spreads = {'g_ffn': (-1.0, 0.6),
     'L0_xattn_bq': (0.0, 0.519),
     'L0_xattn_bk': (0.0, 2.0),
     'L0_xattn_bv': (0.0, 0.1),
     'L0_ffn_b1': (0.0, 0.1),
     'L0_ffn_b2': (0.0, 0.1),
     'L1_xattn_bq': (0.0, 0.515),
     'L1_xattn_bk': (0.0, 2.0),
     'L1_xattn_bv': (0.0, 0.1),
     'L1_xattn_bo': (0.0, 0.1),
     'L1_ffn_ln_gamma': (1.0, 0.6),
     'L1_ffn_ln_beta': (0.0, 0.8),
     'L1_ffn_b1': (0.0, 0.8),
     'L1_ffn_b2': (0.0, 0.549)}
    factors = {'L0_ffn_quantum_phases': 23.232,
     'L0_ffn_quantum_weights_real': 51.994,
     'L0_ffn_quantum_weights_imag': 8.0,
     'L1_ffn_mu': 64.0}
    for name, (base, spread) in spreads.items():
        noise = np.random.default_rng([zlib.crc32(name.encode()), seed]).standard_normal(out[name].shape)
        drawn = base * np.exp(spread * noise) if base else spread * noise
        out[name] = jnp.asarray(drawn.astype(out[name].dtype))
    for name, factor in factors.items():
        out[name] = (out[name] * factor).astype(out[name].dtype)
    return out
```

```python
from contextlib import ExitStack

import concourse.bass as bass
from concourse import mybir

F32 = mybir.dt.float32
F32R = mybir.dt.float32r
BF16 = mybir.dt.bfloat16
FP16 = mybir.dt.float16
ALU = mybir.AluOpType
ACT = mybir.ActivationFunctionType
AX = mybir.AxisListType

P = 128
B, S, D = 4, 512, 256
H = 16
DH = D // H
TOK = B * S
NT = TOK // P
QT = S // P
KC = D // P
F = 1024
FT = F // P
E_, SL, HID = 16, 16, 64
ES = E_ * SL
MAXLEN = 125
REL = 2 * MAXLEN - 1
LN_EPS = 1e-5
NORM_EPS = 1e-12
TWO_PI = 6.283185307179586
SIN_SCALE = 6.283185
ROUND = 12582912.0
LOWEST = -3.0e38

TERMS = 6
KROWS = TERMS * DH
KALL = KROWS + 2
VW = 1 + 3 * DH
VLO = 1 + 2 * DH
STACKS = 4
AHEAD = 6
RING = 2 * QT
LAG = 6
SHIFT = 8.0
UNITS = H * B
BODY = STACKS * B
SLAB = S + QT * P - P
EXT = 1024


def two_pi_parts():
    import numpy as np
    hi = np.float32(6.28125)
    mid = np.float32(np.float32((TWO_PI - float(hi)) * 2 ** 20) // 1 / 2 ** 20)
    low = np.float32(TWO_PI - float(hi) - float(mid))
    return float(hi), float(mid), float(low)


class Core:

    def __init__(self, nc, ctx):
        self.nc, self.ctx = nc, ctx
        self.sems = []

    def sem(self, name):
        self.sems.append(self.nc.alloc_semaphore(name=name))
        return self.sems[-1]

    def clear_sems(self):
        with self.nc.Block() as block:
            @block.gpsimd
            def _(pool):
                for sem in self.sems:
                    pool.sem_clear(sem)
        for sem in self.sems:
            self.nc.release_semaphore(sem)
        self.sems = []

    def sb(self, name, shape, dt=F32):
        return self.ctx.enter_context(self.nc.sbuf_tensor(name, shape, dt))


def row(ap):
    return ap.rearrange("(a n) -> a n", a=1).to_broadcast([P, ap.shape[0]])


def tile_of(ap, t):
    return ap[:, t, :].rearrange("p a d -> p (a d)")


def column(ap):
    return ap.rearrange("(i p) -> p i", p=P)


def load_phase(k, a):
    nc = k.nc
    s = k.sem
    loaded, rel_loaded, gates_loaded, theta_loaded = s("ld_inputs"), s("ld_rel"), s("ld_gates"), s("ld_theta")
    ctx_in, x_in = [s(f"ld_ctx{b}") for b in range(B)], [s(f"ld_x{b}") for b in range(B)]
    ctx_turned, ctx_taken = s("ld_ctxturned"), s("ld_ctxtaken")
    zeroed, diag, ident_done = s("ld_zeroed"), s("ld_diag"), s("ld_ident")
    ext_zero, ext_done, ext_stored = s("ld_extzero"), s("ld_extdone"), s("ld_extstored")
    chain, sin_in, sin_out, tanh_done = s("ld_chain"), s("ld_sinin"), s("ld_sinout"), s("ld_tanh")
    stats = s("ld_stats")
    wt_ready, wt_taken = s("ld_wtready"), s("ld_wttaken")
    c1, c2, c3 = two_pi_parts()
    with ExitStack() as local:
        def sb(name, shape, dt=F32):
            return local.enter_context(nc.sbuf_tensor(name, shape, dt))
        rel = sb("rel", [H, REL])
        ext = sb("ext", [H, EXT])
        wraw = sb("wraw", [P, 4, KC, D])
        turned = [local.enter_context(nc.psum_tensor(f"turned{i}", [P, 512], F32)) for i in range(4)]
        th = sb("th", [P, FT])
        tb1 = sb("tb1", [P, FT])
        wr = sb("wr", [P, FT])
        wi = sb("wi", [P, FT])
        turns = sb("turns", [P, FT])
        whole = sb("whole", [P, FT])
        rem = [sb(f"rem{i}", [P, FT]) for i in range(3)]
        quarter = sb("quarter", [P, FT])
        sc = sb("sc", [P, 2, FT])
        half = sb("halfs", [P, 2, FT])
        prod = sb("prod", [P, 3, FT])
        graw = sb("graw", [P, 4])
        antif = sb("antif", [P, P])
        cbank = [local.enter_context(nc.psum_tensor(f"cbank{i}", [P, S], F32)) for i in range(4)]
        LOADS = 16 * 17
        with nc.Block() as block:
            @block.sync
            def _(sp):
                sp.dma_start(rel[:, :], a["L0_xattn_rel_emb"]).then_inc(rel_loaded, 16)
                for b in range(B):
                    sp.dma_start(k.ctxin[:, QT * b:QT * b + QT, :],
                                 a["ctx_1024"][b].rearrange("(t p) d -> p t d", p=P)).then_inc(ctx_in[b], 16)
                for b in range(B):
                    sp.dma_start(k.x[:, QT * b:QT * b + QT, :],
                                 a["x"][b].rearrange("(t p) d -> p t d", p=P)).then_inc(x_in[b], 16)
                for n, w in enumerate(("Wq", "Wk", "Wv")):
                    sp.dma_start(k.w0[:, n], a["L0_xattn_" + w].rearrange("(c p) o -> p c o", p=P)).then_inc(loaded, 16)
                for n, w in enumerate(("Wq", "Wk", "Wv", "Wo")):
                    sp.dma_start(wraw[:, n], a["L1_xattn_" + w].rearrange("(c p) i -> p c i", p=P)).then_inc(loaded, 16)
                for layer in range(2):
                    sp.dma_start(k.bvb[:, layer, :], row(a[f"L{layer}_xattn_bv"])).then_inc(loaded, 16)
                sp.dma_start(k.bob[:, :], row(a["L1_xattn_bo"])).then_inc(loaded, 16)
                sp.dma_start(k.b2b[:, :], row(a["L0_ffn_b2"])).then_inc(loaded, 16)
                sp.wait_ge(ext_done, 6)
                sp.dma_start(k.ext_dram.ap(), ext[:, :]).then_inc(ext_stored, 16)
                sp.wait_ge(ext_stored, 16)
                sp.wait_ge(loaded, LOADS)

            @block.scalar
            def _(act):
                with nc.allow_non_contiguous_dma(reason="small bias vectors, one number a partition"):
                    act.dma_start(graw[:, 0:2], row(a["g_xattn"])).then_inc(gates_loaded, 16)
                    act.dma_start(graw[:, 2:4], row(a["g_ffn"])).then_inc(gates_loaded, 16)
                    act.dma_start(th[:, :], column(a["L0_ffn_quantum_phases"])).then_inc(theta_loaded, 16)
                    act.dma_start(wr[:, :], column(a["L0_ffn_quantum_weights_real"])).then_inc(theta_loaded, 16)
                    act.dma_start(wi[:, :], column(a["L0_ffn_quantum_weights_imag"])).then_inc(theta_loaded, 16)
                    act.dma_start(k.b1c[:, :], column(a["L0_ffn_b1"])).then_inc(theta_loaded, 16)
                    for layer in range(2):
                        for n, w in enumerate(("bq", "bk")):
                            act.dma_start(k.bqk[:, layer, n, :], column(a[f"L{layer}_xattn_{w}"])).then_inc(loaded, 16)
                    act.dma_start(k.scale[:, :], row(a["L1_ffn_scale"])).then_inc(loaded, 16)
                    act.dma_start(k.b1e[:, :], a["L1_ffn_b1"].rearrange("e h -> h e")).then_inc(loaded, 16)
                def take_ctx(b):
                    for c in range(KC):
                        act.wait_ge(ctx_turned, b * KC + c + 1)
                        act.activation(k.ctxT[:, c, b * S:b * S + S], cbank[b % 2 * KC + c][:, :], ACT.Copy)\
                            .then_inc(ctx_taken, 1)

                act.wait_ge(gates_loaded, 32)
                act.activation(k.gate[:, :], graw[:, :], ACT.Tanh).then_inc(tanh_done, 1)
                act.wait_ge(sin_in, 1)
                act.activation(sc[:, 0, :], half[:, 0, :], ACT.Sin, scale=SIN_SCALE).then_inc(sin_out, 1)
                act.activation(sc[:, 1, :], half[:, 1, :], ACT.Sin, scale=SIN_SCALE).then_inc(sin_out, 1)
                for b in range(B):
                    take_ctx(b)
                for n in range(4):
                    act.wait_ge(wt_ready, n + 1)
                    act.activation(k.wt1[:, n, :, :], turned[n][:, :].rearrange("p (c o) -> p c o", c=KC),
                                   ACT.Copy).then_inc(wt_taken, 1)

            @block.gpsimd
            def _(pool):
                pool.memset(k.ident[:, :], 0.0).then_inc(zeroed, 1)
                pool.memset(antif[:, :], 0.0).then_inc(zeroed, 1)
                pool.memset(k.ones[:, :], 1.0).then_inc(zeroed, 1)
                pool.wait_ge(zeroed, 3)
                pool.affine_select(out=k.ident[:, :], in_=k.ident[:, :], compare_op=ALU.not_equal, fill=1.0,
                                   base=0, pattern=[[-1, P]], channel_multiplier=1).then_inc(diag, 1)
                pool.affine_select(out=antif[:, :], in_=antif[:, :], compare_op=ALU.not_equal, fill=1.0,
                                   base=1 - P, pattern=[[1, P]], channel_multiplier=1).then_inc(diag, 1)
                pool.wait_ge(diag, 2)
                pool.tensor_scalar(k.anti[:, :], antif[:, :], 1.0, 0.0, ALU.mult, ALU.add).then_inc(ident_done, 1)
                pool.tensor_scalar(k.identb[:, :], k.ident[:, :], 1.0, 0.0, ALU.mult, ALU.add).then_inc(ident_done, 1)
                pool.wait_ge(ident_done, 2)

            @block.tensor
            def _(pe):
                pe.wait_ge(diag, 2)
                for b in range(B):
                    pe.wait_ge(ctx_in[b], 16)
                    if b >= 2:
                        pe.wait_ge(ctx_taken, (b - 1) * KC)
                    for c in range(KC):
                        for j in range(QT):
                            last = pe.transpose(cbank[b % 2 * KC + c][:, j * P:j * P + P],
                                                k.ctxin[:, b * QT + j, c * P:c * P + P], k.ident[:, :])
                        last.then_inc(ctx_turned, 1)
                pe.wait_ge(loaded, LOADS)
                for n in range(4):
                    for ic in range(KC):
                        for oc in range(KC):
                            last = pe.transpose(turned[n][:, ic * D + oc * P:ic * D + oc * P + P],
                                                wraw[:, n, oc, ic * P:ic * P + P], k.ident[:, :])
                    last.then_inc(wt_ready, 1)

            @block.vector
            def _(dve):
                step = [0]

                def then(ins):
                    step[0] += 1
                    ins.then_inc(chain, 1)
                    dve.wait_ge(chain, step[0])

                dve.memset(ext[:, :], 0.0).then_inc(ext_zero, 1)
                dve.wait_ge(ext_zero, 1)
                dve.wait_ge(rel_loaded, 16)
                low = S - 1 - (MAXLEN - 1) - REL
                dve.tensor_scalar(ext[:, 0:low], ext[:, 0:low], rel[:, 0:1], None, ALU.add).then_inc(ext_done, 1)
                dve.tensor_copy(ext[:, low:low + REL], rel[:, :]).then_inc(ext_done, 1)
                dve.tensor_copy(ext[:, low + REL:low + 2 * REL], rel[:, :]).then_inc(ext_done, 1)
                dve.tensor_scalar(ext[:, low + 2 * REL:EXT - 1], ext[:, low + 2 * REL:EXT - 1],
                                  rel[:, REL - 1:REL], None, ALU.add).then_inc(ext_done, 1)
                dve.memset(ext[:, EXT - 1:EXT], 0.0).then_inc(ext_done, 1)
                dve.wait_ge(ext_done, 5)
                dve.tensor_scalar(ext[:, :], ext[:, :], rel[:, REL - 1:REL], None, ALU.subtract).then_inc(ext_done, 1)
                dve.wait_ge(theta_loaded, 64)
                then(dve.tensor_scalar(turns[:, :], th[:, :], 1.0 / TWO_PI, None, ALU.mult))
                then(dve.tensor_scalar(whole[:, :], turns[:, :], ROUND, ROUND, ALU.add, ALU.subtract))
                then(dve.scalar_tensor_tensor(out=rem[0][:, :], in0=whole[:, :], scalar=-c1, in1=th[:, :],
                                              op0=ALU.mult, op1=ALU.add))
                then(dve.scalar_tensor_tensor(out=rem[1][:, :], in0=whole[:, :], scalar=-c2, in1=rem[0][:, :],
                                              op0=ALU.mult, op1=ALU.add))
                then(dve.scalar_tensor_tensor(out=rem[2][:, :], in0=whole[:, :], scalar=-c3, in1=rem[1][:, :],
                                              op0=ALU.mult, op1=ALU.add))
                then(dve.tensor_scalar(half[:, 0, :], rem[2][:, :], 1.0 / TWO_PI, None, ALU.mult))
                then(dve.tensor_scalar(quarter[:, :], half[:, 0, :], 0.25, None, ALU.add))
                then(dve.tensor_scalar(prod[:, 0, :], quarter[:, :], ROUND, ROUND, ALU.add, ALU.subtract))
                then(dve.tensor_tensor(half[:, 1, :], quarter[:, :], prod[:, 0, :], ALU.subtract))
                then(dve.tensor_scalar(half[:, :, :], half[:, :, :], 0.5, -0.5, ALU.min, ALU.max))
                then(dve.tensor_scalar(tb1[:, :], k.b1c[:, :], 0.1 / TWO_PI, None, ALU.mult))
                dve.tensor_tensor(k.phase[:, :], tb1[:, :], half[:, 0, :], ALU.add).then_inc(sin_in, 1)
                dve.wait_ge(sin_out, 2)
                then(dve.tensor_tensor(prod[:, 0, :], sc[:, 1, :], wr[:, :], ALU.mult))
                then(dve.tensor_tensor(prod[:, 1, :], sc[:, 0, :], wi[:, :], ALU.mult))
                then(dve.tensor_tensor(prod[:, 2, :], prod[:, 0, :], prod[:, 1, :], ALU.add))
                then(dve.scalar_tensor_tensor(out=k.coef[:, :], in0=prod[:, 2, :], scalar=0.1, in1=wi[:, :],
                                              op0=ALU.mult, op1=ALU.mult))
                for b in range(B):
                    dve.wait_ge(x_in[b], 16)
                    for t in range(b * QT, b * QT + QT):
                        dve.bn_stats(k.st[:, t, :], k.x[:, t, :]).then_inc(stats, 1)
                dve.wait_ge(loaded, LOADS)
                dve.wait_ge(tanh_done, 1)
                then(dve.tensor_scalar(k.bqk[:, :, 0, :], k.bqk[:, :, 0, :], DH ** -0.5, None, ALU.mult))
                then(dve.tensor_scalar(k.b2b[:, :], k.b2b[:, :], k.gate[:, 2:3], None, ALU.mult))
                then(dve.tensor_scalar(k.bob[:, :], k.bob[:, :], k.gate[:, 1:2], None, ALU.mult))


def turn_phase(k, name, src, dst, loads=None):
    nc = k.nc
    s = lambda n: k.sem(f"{name}_{n}")
    aggr, eps_done, sd_done, rstd_done, normed, turned, taken = map(
        s, ("aggr", "eps", "sd", "rstd", "normed", "turned", "taken"))
    AHEAD_BANKS = 2 * KC
    with ExitStack() as local:
        def sb(n, shape, dt=F32):
            return local.enter_context(nc.sbuf_tensor(f"{name}_{n}", shape, dt))
        mv = sb("mv", [P, NT, 2])
        var = sb("var", [P, NT])
        sd = sb("sd", [P, NT])
        rstd = sb("rstd", [P, NT])
        xn = sb("xn", [P, 2, QT, D])
        bank = [[local.enter_context(nc.psum_tensor(f"{name}_bank{e}{c}", [P, S], F32)) for c in range(KC)]
                for e in range(2)]
        with nc.Block() as block:
            @block.sync
            def _(sp):
                if loads:
                    loads(sp)

            @block.vector
            def _(dve):
                for t in range(NT):
                    dve.bn_aggr(mv[:, t, :], k.st[:, t, :]).then_inc(aggr, 1)
                dve.wait_ge(aggr, NT)
                dve.tensor_scalar(var[:, :], mv[:, :, 1], LN_EPS, None, ALU.add).then_inc(eps_done, 1)
                dve.wait_ge(sd_done, 1)
                dve.reciprocal(rstd[:, :], sd[:, :]).then_inc(rstd_done, 1)
                dve.wait_ge(rstd_done, 1)
                with dve.Fori(0, B // 2) as i:
                    for e in range(2):
                        dve.wait_ge(turned, i * 2 * KC + e * KC + KC)
                        for j in range(QT):
                            t = bass.ds(i * 2 * QT + e * QT + j, 1)
                            dve.tensor_scalar(xn[:, e, j, :], tile_of(src, t), mv[:, t, 0], rstd[:, t],
                                              ALU.subtract, ALU.mult).then_inc(normed, 1)

            @block.scalar
            def _(act):
                act.sem_inc(taken, AHEAD_BANKS)
                act.wait_ge(eps_done, 1)
                act.activation(sd[:, :], var[:, :], ACT.Sqrt).then_inc(sd_done, 1)
                with act.Fori(0, B // 2) as i:
                    for e in range(2):
                        for c in range(KC):
                            act.wait_ge(turned, i * 2 * KC + e * KC + c + 1 + AHEAD_BANKS)
                            act.activation(dst[:, c, bass.ds(i * 2 * S + e * S, S)], bank[e][c][:, :],
                                           ACT.Copy).then_inc(taken, 1)

            @block.tensor
            def _(pe):
                pe.sem_inc(turned, AHEAD_BANKS)
                with pe.Fori(0, B // 2) as i:
                    for e in range(2):
                        pe.wait_ge(normed, i * 2 * QT + e * QT + QT)
                        pe.wait_ge(taken, i * 2 * KC + e * KC + KC)
                        for c in range(KC):
                            for j in range(QT):
                                last = pe.transpose(bank[e][c][:, j * P:j * P + P],
                                                    xn[:, e, j, c * P:c * P + P], k.ident[:, :])
                            last.then_inc(turned, 1)


def project_phase(k, layer):
    nc = k.nc
    s = lambda n: k.sem(f"pr{layer}_{n}")
    made, cut_high, rest_done, mid_done, low_done = map(s, ("made", "cuthigh", "rest", "mid", "low"))
    stored = [s(f"stored{u}") for u in range(2 * KC)]
    v_made, v_sum, v_high, v_rest, v_mid, v_low, v_ones = map(
        s, ("vmade", "vsum", "vhigh", "vrest", "vmid", "vlow", "vones"))
    k.stack_in = [s(f"stack{i}") for i in range(STACKS)]
    wt = [k.w0[:, n] for n in range(3)] if layer == 0 else [k.wt1[:, n] for n in range(3)]
    scale = (DH ** -0.5, 1.0)
    moving = (k.hT, k.ctxT)
    RING = 2 * KC
    VBUF = 4
    with ExitStack() as local:
        def sb(n, shape, dt=F32):
            return local.enter_context(nc.sbuf_tensor(f"pr{layer}_{n}", shape, dt))
        full = sb("full", [P, RING, S])
        rest = sb("rest", [P, RING, S])
        part = sb("part", [P, RING, 3, S], BF16)
        vfull = sb("vfull", [P, VBUF, D])
        vrest = sb("vrest", [P, VBUF, D])
        bank = [local.enter_context(nc.psum_tensor(f"pr{layer}_bank{i}", [P, S], F32)) for i in range(RING)]
        vbank = [local.enter_context(nc.psum_tensor(f"pr{layer}_vbank{i}", [P, D], F32)) for i in range(VBUF)]
        units = [(w, c) for w in range(2) for c in range(KC)]
        heads = lambda ap: ap.rearrange("p (h d) -> p h d", h=H)
        with nc.Block() as block:
            @block.tensor
            def _(pe):
                with pe.Fori(0, B) as b:
                    for u, (w, c) in enumerate(units):
                        pe.wait_ge(cut_high, b * RING + u + 1)
                        for kc in range(KC):
                            last = pe.matmul(bank[u][:, :], wt[w][:, kc, c * P:c * P + P],
                                             moving[w][:, kc, bass.ds(b * S, S)], start=kc == 0, stop=kc == KC - 1)
                        last.then_inc(made, 1)
                for t in range(NT):
                    if t >= VBUF:
                        pe.wait_ge(v_sum, t - VBUF + 1)
                    for kc in range(KC):
                        last = pe.matmul(vbank[t % VBUF][:, :], k.ctxT[:, kc, t * P:t * P + P], wt[2][:, kc, :],
                                         start=kc == 0, stop=kc == KC - 1)
                    last.then_inc(v_made, 1)

            @block.scalar
            def _(act):
                act.sem_inc(cut_high, RING)
                with act.Fori(0, B) as b:
                    for u, (w, c) in enumerate(units):
                        act.wait_ge(made, b * RING + u + 1)
                        act.wait_ge(low_done, b * RING + u + 1)
                        act.wait_ge(stored[u], b * 16 + 16)
                        bias = k.bqk[:, layer, w, c:c + 1]
                        act.activation(full[:, u, :], bank[u][:, :], ACT.Identity, bias=bias, scale=scale[w])
                        act.activation(part[:, u, 0, :], bank[u][:, :], ACT.Identity, bias=bias,
                                       scale=scale[w]).then_inc(cut_high, 1)
                for t in range(NT + 1):
                    if t < NT:
                        act.wait_ge(v_sum, t + 1)
                        act.activation(k.v[:, t, :, 1:1 + DH], heads(vfull[:, t % VBUF, :]), ACT.Copy)\
                            .then_inc(v_high, 1)
                    if t >= 1:
                        u = t - 1
                        act.wait_ge(v_rest, u + 1)
                        act.activation(k.v[:, u, :, 1 + DH:1 + 2 * DH], heads(vrest[:, u % VBUF, :]), ACT.Copy)\
                            .then_inc(v_mid, 1)

            @block.vector
            def _(dve):
                dve.memset(k.v[:, :, :, 0:1], 1.0).then_inc(v_ones, 1)
                with dve.Fori(0, B) as b:
                    for u in range(RING):
                        at = b * RING + u + 1
                        dve.wait_ge(cut_high, at + RING)
                        dve.tensor_tensor(rest[:, u, :], full[:, u, :], part[:, u, 0, :], ALU.subtract)\
                            .then_inc(rest_done, 1)
                        dve.wait_ge(rest_done, at)
                        dve.tensor_copy(part[:, u, 1, :], rest[:, u, :]).then_inc(mid_done, 1)
                for t in range(NT + 2):
                    if t < NT:
                        dve.wait_ge(v_made, t + 1)
                        dve.tensor_tensor(vfull[:, t % VBUF, :], vbank[t % VBUF][:, :], k.bvb[:, layer, :], ALU.add)\
                            .then_inc(v_sum, 1)
                    if 1 <= t <= NT:
                        u = t - 1
                        dve.wait_ge(v_high, u + 1)
                        dve.tensor_tensor(heads(vrest[:, u % VBUF, :]), heads(vfull[:, u % VBUF, :]),
                                          k.v[:, u, :, 1:1 + DH], ALU.subtract).then_inc(v_rest, 1)
                    if t >= 2:
                        u = t - 2
                        dve.wait_ge(v_mid, u + 1)
                        dve.tensor_tensor(k.v[:, u, :, 1 + 2 * DH:VW], heads(vrest[:, u % VBUF, :]),
                                          k.v[:, u, :, 1 + DH:1 + 2 * DH], ALU.subtract).then_inc(v_low, 1)

            @block.gpsimd
            def _(pool):
                pool.sem_inc(low_done, RING)
                with pool.Fori(0, B) as b:
                    for u in range(RING):
                        pool.wait_ge(mid_done, b * RING + u + 1)
                        pool.tensor_tensor(part[:, u, 2, :], rest[:, u, :], part[:, u, 1, :], ALU.subtract)\
                            .then_inc(low_done, 1)

            @block.sync
            def _(sp):
                for u in range(RING):
                    sp.sem_inc(stored[u], 16)
                with sp.Fori(0, B) as b:
                    for u, (w, c) in enumerate(units):
                        sp.wait_ge(low_done, b * RING + u + 1 + RING)
                        sp.dma_start(k.parts[w].ap()[:, c * P:c * P + P, bass.ds(b * S, S)].rearrange("n p t -> p n t"),
                                     part[:, u, :, :]).then_inc(stored[u], 16)
                for u in range(RING):
                    sp.wait_ge(stored[u], 16 * (B + 1))
                for head in range(STACKS):
                    load_stacks(k, sp, layer, head, head)


def load_stacks(k, sp, layer, head, buf):
    h = bass.ds(head * DH, DH)
    qp, kp = (k.parts[w].ap() for w in range(2))
    for dst, src in ((k.qs[0:3 * DH], qp[0:3, h, :]), (k.qs[3 * DH:5 * DH], qp[0:2, h, :]),
                     (k.qs[5 * DH:6 * DH], qp[0:1, h, :]),
                     (k.ks[0:3 * DH], kp[0:1, h, :].to_broadcast([3, DH, TOK])),
                     (k.ks[3 * DH:5 * DH], kp[1:2, h, :].to_broadcast([2, DH, TOK])),
                     (k.ks[5 * DH:6 * DH], kp[2:3, h, :])):
        sp.dma_start(dst[:, buf, :], src).then_inc(k.stack_in[buf], 16)
    if layer == 0:
        r = k.ext_dram.ap()[bass.ds(head, 1), :]
        sp.dma_start(k.slab[:, buf, :], bass.AP(k.ext_dram, r.offset, [[1, P], [1, SLAB]]))\
            .then_inc(k.stack_in[buf], 16)


def attention_phase(k, layer):
    nc = k.nc
    s = lambda n: k.sem(f"at{layer}_{n}")
    biased = layer == 0
    MG = 2
    MGU = QT // MG

    def on_dve(d, kt):
        return kt == 0 or kt == 2 and d % 2 == 0

    def place(d, kt, dve):
        upto = [(u, t) for u in range(d + 1) for t in range(QT) if (u, t) <= (d, kt)]
        return sum(on_dve(*tile) == dve for tile in upto)

    max_made, max_taken, scores_made, exp_done = map(s, ("maxmade", "maxtaken", "scores", "exp"))
    lo_dve, lo_pool, pv_done, out_taken = map(s, ("lodve", "lopool", "pv", "outtaken"))
    neg_full, neg_high, neg_parts, neg_turned, neg_copied = map(
        s, ("negfull", "neghigh", "negparts", "negturned", "negcopied"))
    ones_done = s("ones")
    stack_in, qs, ks = k.stack_in, k.qs, k.ks
    neg_in = [s(f"neg{i}") for i in range(2)]
    slab_high, slab_low = s("slabhigh"), s("slablow")
    LOADS = 6 + biased
    with ExitStack() as local:
        def sb(n, shape, dt=F32):
            return local.enter_context(nc.sbuf_tensor(f"at{layer}_{n}", shape, dt))
        prob = sb("prob", [P, 2, QT, S])
        remn = sb("remn", [P, 2, QT, S], FP16)
        mx = sb("mx", [P, 2, NT])
        negf = sb("negf", [P, 2, NT])
        neg = sb("neg", [P, 2, 2, NT], BF16)
        negT = sb("negT", [2 * NT, 2, P], BF16)
        if biased:
            slab = k.slab
            tick = sb("tick", [P, 2])
            slabh = sb("slabh", [P, 2, SLAB], F32R)
            slabl = sb("slabl", [P, 2, SLAB], F32R)
        mbank = [local.enter_context(nc.psum_tensor(f"at{layer}_mb{i}", [P, MG, S], F32)) for i in range(2)]
        sbank = [local.enter_context(nc.psum_tensor(f"at{layer}_sb{i}", [P, S], F32)) for i in range(2)]
        obank = [local.enter_context(nc.psum_tensor(f"at{layer}_ob{i}", [P, S], F32)) for i in range(2)]
        high = prob[:, :, :, :].bitcast(BF16)

        def hi(buf, kt, qt):
            return high[:, buf, kt, 2 * qt * P + 1:2 * (qt + 1) * P:2]

        LAST = UNITS // BODY - 1

        def slots(eng, slot):
            for c in range(2):
                slot(0, c, True, True)
            with eng.Fori(0, LAST) as i:
                for c in range(2, BODY + 2):
                    slot(i, c, True, True)
            for c in range(2, BODY + 2):
                slot(LAST, c, c < BODY, c + AHEAD < BODY)

        def negates(i, c):
            return c % B == 2 and (not isinstance(i, int) or i * STACKS + (c + 2) // B < H)

        def neg_head(i, c):
            return i * STACKS + (c + 2) // B

        with nc.Block() as block:
            @block.sync
            def _(sp):
                def neg_rows(a, buf):
                    sp.wait_ge(neg_copied, a + 1)
                    for n in range(2):
                        sp.dma_start(qs[KROWS + n:KROWS + n + 1, buf, :], negT[n * NT:n * NT + NT, buf % 2, :])\
                            .then_inc(neg_in[buf % 2], 16)

                neg_rows(0, 0)
                with sp.Fori(0, LAST) as i:
                    for c in range(1, STACKS + 1):
                        neg_rows(i * STACKS + c, c % STACKS)
                        sp.wait_ge(scores_made, i * (STACKS * B * QT) + c * B * QT)
                        load_stacks(k, sp, layer, i * STACKS + c + STACKS - 1, (c - 1) % STACKS)
                for c in range(1, STACKS):
                    neg_rows(LAST * STACKS + c, c)

            @block.tensor
            def _(pe):
                pe.sem_inc(pv_done, RING)

                def maxima(i, d, j):
                    buf, b = d // B % STACKS, d % B
                    if b == 0 and j == 0:
                        pe.wait_ge(stack_in[buf], i * (LOADS * 16) + (d // BODY + 1) * LOADS * 16)
                    g, m = divmod(j, MG)
                    if m == 0:
                        pe.wait_ge(max_taken, i * (BODY * MGU) + d * MGU + g + 1)
                    mm = pe.matmul(mbank[g % 2][:, m, :], qs[0:KROWS, buf, b * S + j * P:b * S + j * P + P],
                                   ks[0:KROWS, buf, b * S:b * S + S], start=True, stop=True)
                    if m == MG - 1:
                        mm.then_inc(max_made, 1)

                def scores(i, d, kt):
                    buf, b = d // B % STACKS, d % B
                    if b == 0 and kt == 0:
                        pe.wait_ge(neg_in[buf % 2], i * (STACKS // 2 * 32) + (d // B // 2 + 1) * 32)
                        if biased:
                            pe.wait_ge(slab_low, i * STACKS + d // B + 1)
                    pe.wait_ge(exp_done, i * (BODY * QT) + d * QT + kt + 1)
                    mm = pe.matmul(sbank[kt % 2][:, :], ks[0:KALL, buf, b * S + kt * P:b * S + kt * P + P],
                                   qs[0:KALL, buf, b * S:b * S + S], start=True, stop=True)
                    if biased:
                        x0, n = (QT - 1 - kt) * P, min(QT, kt + 2) * P
                        pe.matmul(sbank[kt % 2][:, 0:n], k.anti[:, :], slabh[:, buf % 2, x0:x0 + n],
                                  start=False, stop=True, skip_group_check=True)
                        mm = pe.matmul(sbank[kt % 2][:, 0:n], k.anti[:, :], slabl[:, buf % 2, x0:x0 + n],
                                       start=False, stop=True, skip_group_check=True)
                    mm.then_inc(scores_made, 1)

                def values(i, d, kt):
                    buf, b = d % 2, d % B
                    if on_dve(d, kt):
                        pe.wait_ge(lo_dve, i * place(BODY - 1, QT - 1, True) + place(d, kt, True))
                    else:
                        pe.wait_ge(lo_pool, i * place(BODY - 1, QT - 1, False) + place(d, kt, False))
                    if kt == 0:
                        pe.wait_ge(out_taken, i * BODY + d + 1)
                        if negates(i, d) or d == 0:
                            pe.wait_ge(neg_copied, i * STACKS + (d + 2) // B + 1)
                    h = bass.ds(i * STACKS + d // B, 1)
                    for qt in range(QT):
                        pe.matmul(obank[buf][:, qt * 64:qt * 64 + VW], hi(buf, kt, qt), k.v[:, b * QT + kt, h, :],
                                  start=kt == 0 and qt == 0, stop=False, skip_group_check=True)
                        mm = pe.matmul(obank[buf][:, qt * 64:qt * 64 + VLO], remn[:, buf, kt, qt * P:qt * P + P],
                                       k.v[:, b * QT + kt, h, 0:VLO], start=False, stop=kt == QT - 1,
                                       skip_group_check=True)
                    mm.then_inc(pv_done, 1)

                def turn_neg(a, buf):
                    pe.wait_ge(neg_parts, a + 1)
                    pe.transpose(obank[0][:, :].bitcast(BF16)[0:2 * NT, S:S + P],
                                 neg[:, buf, :, :].rearrange("p n t -> p (n t)"), k.identb[:, :])\
                        .then_inc(neg_turned, 1)

                pe.wait_ge(ones_done, 1)
                for d in range(AHEAD):
                    for j in range(QT):
                        maxima(0, d, j)
                    if d == B:
                        turn_neg(0, 0)

                def slot(i, c, now, ahead):
                    for j in range(QT):
                        if now:
                            scores(i, c, j)
                        if ahead:
                            maxima(i, c + AHEAD, j)
                        d, kt = divmod(c * QT + j - LAG, QT)
                        if 0 <= d < BODY or c >= BODY and now:
                            values(i, d, kt)
                    if negates(i, c):
                        pe.wait_ge(out_taken, i * BODY + c + 1)
                        turn_neg(neg_head(i, c), (c + 2) // B % 2)
                slots(pe, slot)

            @block.scalar
            def _(act):
                act.sem_inc(exp_done, 2)
                act.sem_inc(out_taken, 2)

                def exp(i, d, kt):
                    act.wait_ge(pv_done, i * (BODY * QT) + d * QT + kt + 1)
                    act.wait_ge(scores_made, i * (BODY * QT) + d * QT + kt + 1)
                    act.activation(prob[:, d % 2, kt, :], sbank[kt % 2][:, :], ACT.Exp).then_inc(exp_done, 1)

                def take_out(i, d):
                    act.wait_ge(pv_done, i * (BODY * QT) + (d + 1) * QT + RING)
                    b = d % B
                    act.activation(k.oraw[:, b * QT:b * QT + QT, bass.ds(i * STACKS + d // B, 1), :]
                                   .rearrange("p t h w -> p t (h w)"),
                                   obank[d % 2][:, 0:QT * 64].rearrange("p (t w) -> p t w", w=64)[:, :, 0:VW],
                                   ACT.Copy).then_inc(out_taken, 1)

                def copy_neg(a, buf):
                    act.wait_ge(neg_turned, a + 1)
                    act.activation(negT[:, buf, :], obank[0][:, :].bitcast(BF16)[0:2 * NT, S:S + P],
                                   ACT.Copy).then_inc(neg_copied, 1)

                copy_neg(0, 0)

                def slot(i, c, now, ahead):
                    for kt in range(QT):
                        if now:
                            exp(i, c, kt)
                        if kt == 2 and c >= 2:
                            take_out(i, c - 2)
                    if negates(i, c):
                        copy_neg(neg_head(i, c), (c + 2) // B % 2)
                slots(act, slot)

            @block.vector
            def _(dve):
                dve.sem_inc(max_taken, 2)

                def maxima(i, d, g):
                    dve.wait_ge(max_made, i * (BODY * MGU) + d * MGU + g + 1)
                    buf, t = d // B % 2, d % B * QT + g * MG
                    if biased:
                        dve.memset(tick[:, g:g + 1], 0.0)
                        for m in range(MG):
                            end = (g * MG + m) * P + S
                            last = slab[:, d // B % STACKS, end - 1:end]
                            back = bass.AP(slab, last.offset, [list(last.ap[0]), [-1, S]])
                            ins = dve.tensor_tensor_reduce(out=mbank[g % 2][:, m, :], in0=mbank[g % 2][:, m, :],
                                                           in1=back, scale=1.0, scalar=LOWEST, op0=ALU.add,
                                                           op1=ALU.max, accum_out=mx[:, buf, t + m:t + m + 1])
                        ins.then_inc(max_taken, 1)
                    else:
                        dve.tensor_reduce(mx[:, buf, t:t + MG], mbank[g % 2][:, :, :], AX.X, ALU.max)\
                            .then_inc(max_taken, 1)

                def negate(a, i, c, buf):
                    dve.wait_ge(max_taken, i * (BODY * MGU) + (c + AHEAD) * MGU + 2)
                    dve.tensor_scalar(negf[:, buf, :], mx[:, buf, :], -1.0, SHIFT, ALU.mult, ALU.add)\
                        .then_inc(neg_full, 1)
                    dve.wait_ge(neg_full, a + 1)
                    dve.tensor_copy(neg[:, buf, 0, :], negf[:, buf, :]).then_inc(neg_high, 1)
                    dve.wait_ge(neg_high, a + 1)
                    dve.tensor_tensor(neg[:, buf, 1, :], negf[:, buf, :], neg[:, buf, 0, :], ALU.subtract)\
                        .then_inc(neg_parts, 1)

                def remainder(i, d, kt):
                    dve.wait_ge(exp_done, i * (BODY * QT) + d * QT + kt + 1 + 2)
                    dve.tensor_tensor(remn[:, d % 2, kt, :], prob[:, d % 2, kt, :], high[:, d % 2, kt, 1::2],
                                      ALU.subtract).then_inc(lo_dve, 1)

                dve.memset(ks[KROWS:KALL, :, :], 1.0).then_inc(ones_done, 1)
                for d in range(AHEAD):
                    for g in range(MGU):
                        maxima(0, d, g)
                    if d == B - 1:
                        negate(0, 0, B - AHEAD, 0)

                def slot(i, c, now, ahead):
                    if negates(i, c):
                        negate(neg_head(i, c), i, c, (c + 2) // B % 2)
                    for g in range(MGU):
                        if ahead:
                            maxima(i, c + AHEAD, g)
                        for kt in range(g * MG, g * MG + MG):
                            if now and on_dve(c, kt):
                                remainder(i, c, kt)
                slots(dve, slot)

            @block.gpsimd
            def _(pool):
                def wait_slab(i, d):
                    pool.wait_ge(stack_in[d // B % STACKS], i * (LOADS * 16) + (d // BODY + 1) * LOADS * 16)
                    if d // B > 1:
                        pool.wait_ge(scores_made, i * (BODY * QT) + (d // B - 1) * B * QT)

                def cut_slab(i, d):
                    buf, a = d // B % STACKS, i * STACKS + d // B
                    pool.tensor_scalar(slabh[:, buf % 2, :], slab[:, buf, :], 1.0, 0.0, ALU.mult, ALU.add)\
                        .then_inc(slab_high, 1)
                    pool.wait_ge(slab_high, a + 1)
                    pool.tensor_tensor(slabl[:, buf % 2, :], slab[:, buf, :], slabh[:, buf % 2, :],
                                       ALU.subtract).then_inc(slab_low, 1)

                def remainders(i, d):
                    for kt in range(QT):
                        if not on_dve(d, kt):
                            pool.wait_ge(exp_done, i * (BODY * QT) + d * QT + kt + 1 + 2)
                            pool.tensor_tensor(remn[:, d % 2, kt, :], prob[:, d % 2, kt, :],
                                               high[:, d % 2, kt, 1::2], ALU.subtract).then_inc(lo_pool, 1)

                if biased:
                    wait_slab(0, 0)
                    cut_slab(0, 0)

                def slot(i, c, now, ahead):
                    slab_due = biased and c % B == 0 and (i is not LAST or c + B < BODY)
                    if slab_due:
                        wait_slab(i, c + B)
                    if now:
                        remainders(i, c)
                    if slab_due:
                        cut_slab(i, c + B)
                slots(pool, slot)


PAIR = 2


class Combine:

    def __init__(self, k, name, local, gated):
        s = lambda n: k.sem(f"{name}_{n}")
        self.k, self.gated = k, gated
        self.rec_done, self.small_done, self.whole_done, self.out_done = map(s, ("rec", "small", "whole", "out"))
        sb = lambda n, shape: local.enter_context(k.nc.sbuf_tensor(f"{name}_{n}", shape, F32))
        self.small = sb("small", [P, 2, PAIR, H, DH])
        self.whole = sb("whole", [P, 3, PAIR, H, DH])
        self.out = sb("out", [P, 3, PAIR, D])
        self.rec = sb("rec", [P, NT, H])

    def part(self, n, n_of):
        return self.k.oraw[:, n * PAIR:n * PAIR + PAIR, :, 1 + n_of * DH:1 + (n_of + 1) * DH]

    def pool_steps(self, pool, biased=None, bias=None):
        for n in range(NT // PAIR):
            if n >= 2:
                pool.wait_ge(self.whole_done, n - 1)
            pool.tensor_tensor(self.small[:, n % 2], self.part(n, 1), self.part(n, 2), ALU.add)\
                .then_inc(self.small_done, 1)
            if biased is not None:
                xs = self.k.x[:, n * PAIR:n * PAIR + PAIR, :]
                pool.tensor_tensor(xs, xs, bias[:, :].unsqueeze(1).to_broadcast([P, PAIR, D]), ALU.add)\
                    .then_inc(biased, 1)

    def reciprocals(self, dve):
        dve.reciprocal(self.rec[:, :, :], self.k.oraw[:, :, :, 0]).then_inc(self.rec_done, 1)
        dve.wait_ge(self.rec_done, 1)
        if self.gated:
            dve.tensor_scalar(self.rec[:, :, :], self.rec[:, :, :], self.k.gate[:, 0:1], None, ALU.mult)\
                .then_inc(self.rec_done, 1)
            dve.wait_ge(self.rec_done, 2)

    def dve_add(self, dve, n):
        dve.wait_ge(self.small_done, n + 1)
        if n >= 3:
            dve.wait_ge(self.out_done, n - 2)
        dve.tensor_tensor(self.whole[:, n % 3], self.part(n, 0), self.small[:, n % 2], ALU.add)\
            .then_inc(self.whole_done, 1)

    def dve_divide(self, dve, n):
        dve.wait_ge(self.whole_done, n + 1)
        rec = self.rec[:, n * PAIR:n * PAIR + PAIR, :].unsqueeze(3).to_broadcast([P, PAIR, H, DH])
        dve.tensor_tensor(self.out[:, n % 3].rearrange("p t (h d) -> p t h d", h=H), self.whole[:, n % 3],
                          rec, ALU.mult).then_inc(self.out_done, 1)


def residual0_phase(k):
    nc = k.nc
    added, stats = k.sem("r0_added"), k.sem("r0_stats")
    with ExitStack() as local:
        comb = Combine(k, "r0", local, True)
        with nc.Block() as block:
            @block.gpsimd
            def _(pool):
                comb.pool_steps(pool)

            @block.vector
            def _(dve):
                comb.reciprocals(dve)
                STEPS = NT // PAIR
                for n in range(STEPS + 3):
                    if n < STEPS:
                        comb.dve_add(dve, n)
                    if 2 <= n <= STEPS + 1:
                        u = n - 2
                        dve.wait_ge(comb.out_done, u + 1)
                        dve.tensor_tensor(k.x[:, u * PAIR:u * PAIR + PAIR, :], comb.out[:, u % 3],
                                          k.x[:, u * PAIR:u * PAIR + PAIR, :], ALU.add).then_inc(added, 1)
                    if 1 <= n <= STEPS:
                        if n >= 4:
                            dve.wait_ge(added, n - 3)
                        comb.dve_divide(dve, n - 1)
                    if n >= 3:
                        dve.wait_ge(added, n - 2)
                        for t in range((n - 3) * PAIR, (n - 2) * PAIR):
                            dve.bn_stats(k.st[:, t, :], k.x[:, t, :]).then_inc(stats, 1)


def residual1_phase(k):
    nc = k.nc
    turned, turned_out, made, added, biased, stats = (
        k.sem("r1_" + n) for n in ("turned", "turnedout", "made", "added", "biased", "stats"))
    STEPS = NT // PAIR
    with ExitStack() as local:
        comb = Combine(k, "r1", local, False)
        oT = local.enter_context(nc.sbuf_tensor("r1_oT", [P, 2, PAIR, KC, P], F32))
        tb = [local.enter_context(nc.psum_tensor(f"r1_tb{i}", [P, PAIR, KC, P], F32)) for i in range(2)]
        yb = [local.enter_context(nc.psum_tensor(f"r1_yb{i}", [P, PAIR, D], F32)) for i in range(2)]
        with nc.Block() as block:
            @block.vector
            def _(dve):
                comb.reciprocals(dve)
                for n in range(STEPS + 4):
                    if n < STEPS:
                        comb.dve_add(dve, n)
                    if 1 <= n <= STEPS:
                        if n >= 4:
                            dve.wait_ge(turned, n - 3)
                        comb.dve_divide(dve, n - 1)
                    if 3 <= n <= STEPS + 2:
                        u = n - 3
                        dve.wait_ge(made, u + 1)
                        dve.wait_ge(biased, u + 1)
                        xs = k.x[:, u * PAIR:u * PAIR + PAIR, :]
                        dve.scalar_tensor_tensor(out=xs, in0=yb[u % 2][:, :, :], scalar=k.gate[:, 1:2], in1=xs,
                                                 op0=ALU.mult, op1=ALU.add).then_inc(added, 1)
                    if n >= 4:
                        dve.wait_ge(added, n - 3)
                        for t in range((n - 4) * PAIR, (n - 3) * PAIR):
                            dve.bn_stats(k.st[:, t, :], k.x[:, t, :]).then_inc(stats, 1)

            @block.gpsimd
            def _(pool):
                comb.pool_steps(pool, biased, k.bob)

            @block.scalar
            def _(act):
                for n in range(STEPS):
                    act.wait_ge(turned, n + 1)
                    if n >= 2:
                        act.wait_ge(made, n - 1)
                    act.activation(oT[:, n % 2], tb[n % 2][:, :, :, :], ACT.Copy).then_inc(turned_out, 1)

            @block.tensor
            def _(pe):
                for n in range(STEPS + 1):
                    if n < STEPS:
                        pe.wait_ge(comb.out_done, n + 1)
                        if n >= 2:
                            pe.wait_ge(turned_out, n - 1)
                        for m in range(PAIR):
                            for c in range(KC):
                                last = pe.transpose(tb[n % 2][:, m, c, :], comb.out[:, n % 3, m, c * P:c * P + P],
                                                    k.ident[:, :])
                        last.then_inc(turned, 1)
                    if n >= 1:
                        u = n - 1
                        pe.wait_ge(turned_out, u + 1)
                        if u >= 2:
                            pe.wait_ge(added, u - 1)
                        for m in range(PAIR):
                            for c in range(KC):
                                last = pe.matmul(yb[u % 2][:, m, :], oT[:, u % 2, m, c, :], k.wt1[:, 3, c, :],
                                                 start=c == 0, stop=c == KC - 1)
                        last.then_inc(made, 1)


def ffn_phase(k):
    nc = k.nc
    s = lambda n: k.sem("ff_" + n)
    h_made, turns_done, whole_done, frac_done, sin_done, mixed, act_done, y_made, y_taken, b2_added, stats = map(
        s, ("hmade", "turns", "whole", "frac", "sin", "mixed", "act", "ymade", "ytaken", "b2added", "stats"))
    with ExitStack() as local:
        def sb(n, shape, dt=F32):
            return local.enter_context(nc.sbuf_tensor("ff_" + n, shape, dt))
        turns, whole, frac, sine, mix, hid = (sb(n, [P, 2, S]) for n in ("turns", "whole", "frac", "sine", "mix", "hid"))
        hb = [local.enter_context(nc.psum_tensor(f"ff_hb{i}", [P, S], F32)) for i in range(4)]
        yb = [local.enter_context(nc.psum_tensor(f"ff_yb{i}", [P, D], F32)) for i in range(QT)]
        with nc.Block() as block:
            @block.tensor
            def _(pe):
                pe.sem_inc(y_made, 2)
                pe.wait_ge(k.ffn_in, 32)
                with pe.Fori(0, B) as b:
                    def hidden(f):
                        pe.wait_ge(mixed, b * FT + f + 1)
                        for c in range(KC):
                            last = pe.matmul(hb[f % 4][:, :], k.w1[:, c, f * P:f * P + P],
                                             k.hT[:, c, bass.ds(b * S, S)], start=c == 0, stop=c == KC - 1)
                        last.then_inc(h_made, 1)

                    def second(f):
                        pe.wait_ge(act_done, b * FT + f + 1)
                        if f == 0:
                            pe.wait_ge(y_taken, b * QT + 1)
                        for j in range(QT):
                            last = pe.matmul(yb[j][:, :], hid[:, f % 2, j * P:j * P + P], k.w2[:, f, :],
                                             start=f == 0, stop=f == FT - 1, skip_group_check=True)
                        last.then_inc(y_made, 1)
                    for f in range(3):
                        hidden(f)
                    for f in range(FT):
                        if f + 3 < FT:
                            hidden(f + 3)
                        second(f)

            @block.scalar
            def _(act):
                with act.Fori(0, B) as b:
                    def sines(f):
                        act.wait_ge(frac_done, b * FT + f + 1)
                        act.activation(sine[:, f % 2, :], frac[:, f % 2, :], ACT.Sin, scale=SIN_SCALE)\
                            .then_inc(sin_done, 1)

                    def relus(f):
                        act.wait_ge(mixed, b * FT + f + 1 + 4)
                        act.wait_ge(y_made, b * FT + f + 1)
                        act.activation(hid[:, f % 2, :], mix[:, f % 2, :], ACT.Relu, bias=k.b1c[:, f:f + 1])\
                            .then_inc(act_done, 1)
                    for f in range(FT + 2):
                        if f < FT:
                            act.wait_ge(h_made, b * FT + f + 1)
                            act.activation(turns[:, f % 2, :], hb[f % 4][:, :], ACT.Identity,
                                           bias=k.phase[:, f:f + 1], scale=0.1 / TWO_PI).then_inc(turns_done, 1)
                        if 1 <= f <= FT:
                            sines(f - 1)
                        if f >= 2:
                            relus(f - 2)

            @block.vector
            def _(dve):
                dve.sem_inc(mixed, 4)
                dve.sem_inc(y_taken, 1)
                with dve.Fori(0, B) as b:
                    def mixes(f):
                        dve.wait_ge(sin_done, b * FT + f + 1)
                        if f >= 2:
                            dve.wait_ge(act_done, b * FT + f - 1)
                        dve.scalar_tensor_tensor(out=mix[:, f % 2, :], in0=sine[:, f % 2, :],
                                                 scalar=k.coef[:, f:f + 1], in1=hb[f % 4][:, :],
                                                 op0=ALU.mult, op1=ALU.add).then_inc(mixed, 1)
                    for f in range(FT + 1):
                        if f < FT:
                            dve.wait_ge(turns_done, b * FT + f + 1)
                            dve.tensor_scalar(whole[:, f % 2, :], turns[:, f % 2, :], ROUND, ROUND,
                                              ALU.add, ALU.subtract).then_inc(whole_done, 1)
                            dve.wait_ge(whole_done, b * FT + f + 1)
                            dve.tensor_tensor(frac[:, f % 2, :], turns[:, f % 2, :], whole[:, f % 2, :],
                                              ALU.subtract).then_inc(frac_done, 1)
                        if f >= 1:
                            mixes(f - 1)
                    dve.wait_ge(y_made, b * FT + FT + 2)
                    dve.wait_ge(b2_added, b * QT + QT)
                    for j in range(QT):
                        t = bass.ds(b * QT + j, 1)
                        xt = tile_of(k.x, t)
                        ins = dve.scalar_tensor_tensor(out=xt, in0=yb[j][:, :], scalar=k.gate[:, 2:3], in1=xt,
                                                       op0=ALU.mult, op1=ALU.add)
                        ins.then_inc(y_taken, 1)
                    for j in range(QT):
                        t = bass.ds(b * QT + j, 1)
                        dve.wait_ge(y_taken, b * QT + j + 2)
                        dve.bn_stats(tile_of(k.st, t), tile_of(k.x, t)).then_inc(stats, 1)

            @block.gpsimd
            def _(pool):
                with pool.Fori(0, B) as b:
                    for j in range(QT):
                        xt = tile_of(k.x, bass.ds(b * QT + j, 1))
                        pool.tensor_tensor(xt, xt, k.b2b[:, :], ALU.add).then_inc(b2_added, 1)


def norm_phase(k, a):
    nc = k.nc
    s = lambda n: k.sem("mn_" + n)
    chain, sqrt_in, sqrt_out, scaled, squares, unit_done, turned, taken = map(
        s, ("chain", "sqrtin", "sqrtout", "scaled", "squares", "unit", "turned", "taken"))
    mu_sq, mu_sum, mu_done = s("musq"), s("musum"), s("mu")
    xn_at, w_in = s("xnat"), s("w")
    with ExitStack() as local:
        def sb(n, shape, dt=F32):
            return local.enter_context(nc.sbuf_tensor("mn_" + n, shape, dt))
        st = sb("st", [P, NT, 6])
        mv = sb("mv", [P, NT, 2])
        mv2 = sb("mv2", [P, NT, 2])
        var = sb("var", [P, 2, NT])
        sd = sb("sd", [P, 2, NT])
        rstd = sb("rstd", [P, 2, NT])
        norm2 = sb("norm2", [P, NT])
        norm = sb("norm", [P, NT])
        unit = sb("unit", [P, NT])
        junk = sb("junk", [P, D])
        xu = sb("xu", [P, 2, QT, D])
        sq = sb("sq", [P, KC, ES])
        munorm = sb("munorm", [P, ES])
        murec = sb("murec", [P, ES])
        mub = local.enter_context(nc.psum_tensor("mn_mub", [P, ES], F32))
        bank = [local.enter_context(nc.psum_tensor(f"mn_bank{i}", [P, S], F32)) for i in range(2 * KC)]
        with nc.Block() as block:
            @block.vector
            def _(dve):
                n = [0]

                def then(*instructions):
                    for ins in instructions:
                        n[0] += 1
                        ins.then_inc(chain, 1)
                    dve.wait_ge(chain, n[0])

                then(*[dve.bn_aggr(mv[:, t, :], k.st[:, t, :]) for t in range(NT)])
                dve.wait_ge(w_in, 48)
                dve.tensor_tensor(sq[:, :, :], k.mu[:, :, :], k.mu[:, :, :], ALU.mult).then_inc(mu_sq, 1)
                for m, (src, mvs) in enumerate(((k.x, mv), (k.xn, mv2))):
                    if m == 1:
                        then(*[dve.bn_stats(st[:, t, :], k.xn[:, t, :]) for t in range(NT)])
                        then(*[dve.bn_aggr(mv2[:, t, :], st[:, t, :]) for t in range(NT)])
                    dve.tensor_scalar(var[:, m, :], mvs[:, :, 1], LN_EPS, None, ALU.add).then_inc(sqrt_in, 1)
                    dve.wait_ge(sqrt_out, m + 1)
                    then(dve.reciprocal(rstd[:, m, :], sd[:, m, :]))
                    then(*[dve.tensor_scalar(k.xn[:, t, :], src[:, t, :], mvs[:, t, 0:1],
                                             rstd[:, m, t:t + 1], ALU.subtract, ALU.mult) for t in range(NT)])
                then(*[dve.tensor_tensor(k.xn[:, t, :], k.xn[:, t, :], k.gamma[:, :], ALU.mult)
                       for t in range(NT)])
                for t in range(NT):
                    dve.tensor_tensor(k.xn[:, t, :], k.xn[:, t, :], k.beta[:, :], ALU.add).then_inc(xn_at, 1)
                dve.wait_ge(sqrt_out, 3)
                then(dve.tensor_scalar(munorm[:, :], munorm[:, :], NORM_EPS, None, ALU.max))
                then(dve.reciprocal(murec[:, :], munorm[:, :]))
                then(*[dve.tensor_tensor(k.mu[:, c, :], k.mu[:, c, :], murec[:, :], ALU.mult) for c in range(KC)])
                dve.wait_ge(sqrt_out, 4)
                then(dve.tensor_scalar(norm[:, :], norm[:, :], NORM_EPS, None, ALU.max))
                then(dve.reciprocal(unit[:, :], norm[:, :]))
                then(dve.tensor_scalar(unit[:, :], unit[:, :], k.scale[:, 0:1], None, ALU.mult))
                for t in range(NT):
                    b, j = divmod(t, QT)
                    if b >= 2 and j == 0:
                        dve.wait_ge(turned, KC * (b - 1))
                    dve.tensor_scalar(xu[:, b % 2, j, :], k.xn[:, t, :], unit[:, t:t + 1], None, ALU.mult)\
                        .then_inc(unit_done, 1)

            @block.scalar
            def _(act):
                for m in range(2):
                    act.wait_ge(sqrt_in, m + 1)
                    act.activation(sd[:, m, :], var[:, m, :], ACT.Sqrt).then_inc(sqrt_out, 1)
                act.wait_ge(mu_sum, 1)
                act.activation(munorm[:, :], mub[:, :], ACT.Sqrt).then_inc(sqrt_out, 1)
                for t in range(NT):
                    act.wait_ge(xn_at, t + 1)
                    if t:
                        act.wait_ge(squares, t)
                    act.activation(junk[:, :], k.xn[:, t, :], ACT.Square, accum_out=norm2[:, t:t + 1])\
                        .then_inc(squares, 1)
                act.wait_ge(squares, NT)
                act.activation(norm[:, :], norm2[:, :], ACT.Sqrt).then_inc(sqrt_out, 1)
                for b in range(B):
                    for c in range(KC):
                        act.wait_ge(turned, b * KC + c + 1)
                        act.activation(k.hT[:, c, b * S:b * S + S], bank[(b % 2) * KC + c][:, :], ACT.Copy)\
                            .then_inc(taken, 1)

            @block.tensor
            def _(pe):
                pe.wait_ge(mu_sq, 1)
                for c in range(KC):
                    last = pe.matmul(mub[:, :], k.ones[:, :], sq[:, c, :], start=c == 0, stop=c == KC - 1)
                last.then_inc(mu_sum, 1)
                for b in range(B):
                    pe.wait_ge(unit_done, b * QT + QT)
                    if b >= 2:
                        pe.wait_ge(taken, (b - 1) * KC)
                    for c in range(KC):
                        for j in range(QT):
                            last = pe.transpose(bank[(b % 2) * KC + c][:, j * P:j * P + P],
                                                xu[:, b % 2, j, c * P:c * P + P], k.ident[:, :])
                        last.then_inc(turned, 1)

            @block.sync
            def _(sp):
                sp.dma_start(k.mu[:, :, :], a["L1_ffn_mu"].rearrange("(c p) e s -> p c (e s)", p=P)).then_inc(w_in, 16)
                sp.dma_start(k.gamma[:, :], row(a["L1_ffn_ln_gamma"])).then_inc(w_in, 16)
                sp.dma_start(k.beta[:, :], row(a["L1_ffn_ln_beta"])).then_inc(w_in, 16)


def experts_phase(k, a, out):
    nc = k.nc
    s = lambda n: k.sem("me_" + n)
    EC = ES // P
    EH = E_ // EC
    lg_made, mx_done, exp_done = map(s, ("logits", "mx", "exp"))
    disp_turned, disp_out, comb_turned, comb_out = map(s, ("dispT", "dispout", "combT", "combout"))
    slot_made, slot_norm, slotT_made, slotT_out = map(s, ("slot", "slotnorm", "slotT", "slotTout"))
    rec_done, sums_done = map(s, ("rec", "sums"))
    hid_made, gelu_done, out_made, out_copied, back = map(s, ("hid", "gelu", "out", "outcopied", "back"))
    stored = [s(f"stored{c}") for c in range(EC)]
    w_in, ones_done, comb_made, added, out_stored = map(s, ("w", "ones", "combmade", "added", "outstored"))
    with ExitStack() as local:
        def sb(n, shape, dt=F32):
            return local.enter_context(nc.sbuf_tensor("me_" + n, shape, dt))

        def ps(n, shape, dt=F32):
            return local.enter_context(nc.psum_tensor("me_" + n, shape, dt))
        ew1 = sb("ew1", [P, KC, E_, HID])
        ew2 = sb("ew2", [HID + 1, E_, D])
        mxs = sb("mxs", [P, B, EC])
        mxt = sb("mxt", [P, B, QT])
        sums = sb("sums", [P, B, EC])
        sumt = sb("sumt", [P, B, QT])
        recs = sb("recs", [P, B, EC])
        rect = sb("rect", [P, B, QT])
        scale = sb("scale", [P, B, QT])
        eslot = sb("eslot", [P, EC, S])
        etok = sb("etok", [P, 2, QT, ES])
        disp = sb("disp", [P, QT, ES])
        comb = sb("comb", [P, B, EC, S])
        slot = sb("slot", [P, EC, D])
        slotT = sb("slotT", [P, KC, E_, B, SL])
        hid = sb("hid", [HID + 1, E_, B * SL])
        eo = sb("eo", [B * SL, E_, D])
        so = sb("so", [P, EC, B, D])
        lgs = ps("lgs", [P, EC, S])
        lgt = ps("lgt", [P, QT, ES])
        tr = ps("tr", [P, 2, 512])
        acc = ps("acc", [P, EC, D])
        tp = ps("tp", [P, KC, EC, P])
        hb = [tr[:, i, :] for i in range(2)]
        ob = [lgs[:, 0, :], lgs[:, 1, :]]
        cb = [tr[:, 0, :], tr[:, 1, :], lgt[:, 0:2, :].rearrange("p a s -> p (a s)"),
              lgt[:, 2:4, :].rearrange("p a s -> p (a s)")]

        with nc.Block() as block:
            @block.tensor
            def _(pe):
                def logits(b):
                    if b:
                        pe.wait_ge(exp_done, 2 * b - 1)
                    for e in range(EC):
                        for c in range(KC):
                            last = pe.matmul(lgs[:, e, :], k.mu[:, c, e * P:e * P + P], k.hT[:, c, b * S:b * S + S],
                                             start=c == 0, stop=c == KC - 1)
                    last.then_inc(lg_made, 1)
                    if b:
                        pe.wait_ge(exp_done, 2 * b)
                    for j in range(QT):
                        t = b * QT + j
                        for c in range(KC):
                            last = pe.matmul(lgt[:, j, :], k.hT[:, c, t * P:t * P + P], k.mu[:, c, :],
                                             start=c == 0, stop=c == KC - 1)
                    last.then_inc(lg_made, 1)

                def turn_slots(b):
                    pe.wait_ge(slot_norm, (b + 1) * EC)
                    if b:
                        pe.wait_ge(slotT_out, b)
                    for e in range(EC):
                        for c in range(KC):
                            last = pe.transpose(tp[:, c, e, :], slot[:, e, c * P:c * P + P], k.ident[:, :])
                    last.then_inc(slotT_made, 1)

                logits(0)
                for b in range(B):
                    pe.wait_ge(exp_done, 2 * b + 1)
                    if b:
                        pe.wait_ge(comb_out, b)
                    for j in range(QT):
                        for e in range(EC):
                            last = pe.transpose(tr[:, j // 2, j % 2 * ES + e * P:j % 2 * ES + e * P + P],
                                                eslot[:, e, j * P:j * P + P], k.ident[:, :])
                    last.then_inc(disp_turned, 1)
                    if b + 1 < B:
                        logits(b + 1)
                    if b:
                        turn_slots(b - 1)
                    pe.wait_ge(exp_done, 2 * b + 2)
                    pe.wait_ge(disp_out, b + 1)
                    for e in range(EC):
                        for j in range(QT):
                            last = pe.transpose(tr[:, e, j * P:j * P + P], etok[:, b % 2, j, e * P:e * P + P],
                                                k.ident[:, :])
                    last.then_inc(comb_turned, 1)
                    if b:
                        pe.wait_ge(slot_norm, b * EC)
                    for e in range(EC):
                        for j in range(QT):
                            last = pe.matmul(acc[:, e, :], disp[:, j, e * P:e * P + P], k.xn[:, b * QT + j, :],
                                             start=j == 0, stop=j == QT - 1)
                        last.then_inc(slot_made, 1)
                turn_slots(B - 1)
                pe.wait_ge(slotT_out, B)
                pe.wait_ge(comb_out, B)
                pe.wait_ge(w_in, 64)
                pe.wait_ge(ones_done, 1)
                for e in range(E_ + 2):
                    if e < E_:
                        if e >= 2:
                            pe.wait_ge(gelu_done, e - 1)
                        for c in range(KC):
                            last = pe.matmul(hb[e % 2][0:HID, 0:B * SL], ew1[:, c, e, :],
                                             slotT[:, c, e, :, :].rearrange("p b s -> p (b s)"),
                                             start=c == 0, stop=c == KC - 1)
                        last.then_inc(hid_made, 1)
                    if e >= 2:
                        u = e - 2
                        pe.wait_ge(gelu_done, u + 1)
                        if u >= 2:
                            pe.wait_ge(out_copied, u - 1)
                        pe.matmul(ob[u % 2][0:B * SL, 0:D], hid[:, u, :], ew2[:, u, :], start=True, stop=True)\
                            .then_inc(out_made, 1)
                pe.wait_ge(gelu_done, E_)
                pe.wait_ge(back, 16 * EC)
                for t in range(NT):
                    b, j = divmod(t, QT)
                    if t >= 4:
                        pe.wait_ge(added, t - 3)
                    for e in range(EC):
                        last = pe.matmul(cb[t % 4][:, 0:D], comb[:, b, e, j * P:j * P + P], so[:, e, b, :],
                                         start=e == 0, stop=e == EC - 1)
                    last.then_inc(comb_made, 1)

            @block.vector
            def _(dve):
                dve.memset(hid[HID:HID + 1, :, :], 1.0).then_inc(ones_done, 1)

                def maxima(b):
                    dve.wait_ge(lg_made, 2 * b + 1)
                    dve.tensor_reduce(mxs[:, b, :], lgs[:, :, :], AX.X, ALU.max, negate=True).then_inc(mx_done, 1)
                    dve.wait_ge(lg_made, 2 * b + 2)
                    dve.tensor_reduce(mxt[:, b, :], lgt[:, :, :], AX.X, ALU.max, negate=True).then_inc(mx_done, 1)
                maxima(0)
                for b in range(B):
                    dve.wait_ge(disp_turned, b + 1)
                    if b:
                        dve.wait_ge(slot_made, b * EC)
                    dve.tensor_copy(disp[:, :, :].rearrange("p j s -> p (j s)"),
                                    tr[:, :, :].rearrange("p a s -> p (a s)")).then_inc(disp_out, 1)
                    dve.reciprocal(recs[:, b, :], sums[:, b, :]).then_inc(rec_done, 1)
                    if b + 1 < B:
                        maxima(b + 1)
                    if b:
                        dve.wait_ge(slotT_made, b)
                    dve.wait_ge(rec_done, b + 1)
                    dve.wait_ge(slot_made, (b + 1) * EC)
                    for e in range(EC):
                        dve.tensor_scalar(slot[:, e, :], acc[:, e, :], recs[:, b, e:e + 1], None, ALU.mult)\
                            .then_inc(slot_norm, 1)
                dve.wait_ge(exp_done, 2 * B)
                dve.reciprocal(rect[:, :, :], sumt[:, :, :]).then_inc(sums_done, 1)
                dve.wait_ge(sums_done, 1)
                dve.tensor_scalar(scale[:, :, :], rect[:, :, :], k.gate[:, 3:4], None, ALU.mult).then_inc(sums_done, 1)
                for e in range(E_):
                    dve.wait_ge(out_made, e + 1)
                    dve.tensor_copy(eo[:, e, :], ob[e % 2][0:B * SL, 0:D]).then_inc(out_copied, 1)
                dve.wait_ge(sums_done, 2)
                for t in range(NT):
                    b, j = divmod(t, QT)
                    dve.wait_ge(comb_made, t + 1)
                    dve.scalar_tensor_tensor(out=k.x[:, t, :], in0=cb[t % 4][:, 0:D], scalar=scale[:, b, j:j + 1],
                                             in1=k.x[:, t, :], op0=ALU.mult, op1=ALU.add).then_inc(added, 1)

            @block.scalar
            def _(act):
                def take_slots(b):
                    act.wait_ge(slotT_made, b + 1)
                    for c in range(KC):
                        last = act.activation(slotT[:, c, :, b, :], tp[:, c, :, :].rearrange("p h (e s) -> p (h e) s", s=SL),
                                              ACT.Copy)
                    last.then_inc(slotT_out, 1)
                for b in range(B):
                    act.wait_ge(mx_done, 2 * b + 1)
                    if b:
                        act.wait_ge(disp_turned, b)
                    for e in range(EC):
                        last = act.activation(eslot[:, e, :], lgs[:, e, :], ACT.Exp, bias=mxs[:, b, e:e + 1],
                                              accum_out=sums[:, b, e:e + 1])
                    last.then_inc(exp_done, 1)
                    act.wait_ge(mx_done, 2 * b + 2)
                    if b >= 2:
                        act.wait_ge(comb_turned, b - 1)
                    for j in range(QT):
                        last = act.activation(etok[:, b % 2, j, :], lgt[:, j, :], ACT.Exp, bias=mxt[:, b, j:j + 1],
                                              accum_out=sumt[:, b, j:j + 1])
                    last.then_inc(exp_done, 1)
                    if b:
                        take_slots(b - 1)
                    act.wait_ge(comb_turned, b + 1)
                    act.activation(comb[:, b, :, :], tr[:, :, :], ACT.Copy).then_inc(comb_out, 1)
                take_slots(B - 1)
                for e in range(E_):
                    act.wait_ge(hid_made, e + 1)
                    act.activation(hid[0:HID, e, :], hb[e % 2][0:HID, 0:B * SL], ACT.Gelu, bias=k.b1e[:, e:e + 1])\
                        .then_inc(gelu_done, 1)

            @block.sync
            def _(sp):
                for c in range(KC):
                    sp.dma_start(ew1[:, c], a["L1_ffn_w1"][:, c * P:c * P + P, :].rearrange("e p h -> p e h"))\
                        .then_inc(w_in, 16)
                sp.dma_start(ew2[0:HID], a["L1_ffn_w2"].rearrange("e h d -> h e d")).then_inc(w_in, 16)
                sp.dma_start(ew2[HID:HID + 1].rearrange("p e d -> p (e d)"),
                             a["L1_ffn_b2"].rearrange("(a e) d -> a (e d)", a=1)).then_inc(w_in, 16)
                for c in range(EC):
                    sp.wait_ge(out_copied, (c + 1) * EH)
                    for b in range(B):
                        sp.dma_start(k.eo_dram.ap()[b, c * P:c * P + P, :].rearrange("(e s) d -> s e d", s=SL),
                                     eo[b * SL:b * SL + SL, c * EH:c * EH + EH, :]).then_inc(stored[c], 16)
                for c in range(EC):
                    sp.wait_ge(stored[c], 16 * B)
                    sp.dma_start(so[:, c], k.eo_dram.ap()[:, c * P:c * P + P, :].rearrange("b p d -> p b d"))\
                        .then_inc(back, 16)
                for t in range(0, NT, 2):
                    sp.wait_ge(added, t + 2)
                    b, j = divmod(t, QT)
                    sp.dma_start(out[b, j * P:(j + 2) * P, :].rearrange("(t p) d -> p t d", p=P), k.x[:, t:t + 2, :])\
                        .then_inc(out_stored, 16)
                sp.wait_ge(out_stored, 16 * NT // 2)


def flamingo_kernel(nc, a, out):
    with ExitStack() as ctx:
        k = Core(nc, ctx)
        k.x = k.sb("x", [P, NT, D])
        k.gate = k.sb("gate", [P, 4])
        k.ident = k.sb("ident", [P, P])
        k.identb = k.sb("identb", [P, P], BF16)
        k.anti = k.sb("anti", [P, P], F32R)
        k.ones = k.sb("ones", [P, P])
        k.wt1 = k.sb("wt1", [P, 4, KC, D])
        k.bqk = k.sb("bqk", [P, 2, 2, KC])
        k.bvb = k.sb("bvb", [P, 2, D])
        k.bob = k.sb("bob", [P, D])
        k.b2b = k.sb("b2b", [P, D])
        k.b1c = k.sb("b1c", [P, FT])
        k.phase = k.sb("phase", [P, FT])
        k.coef = k.sb("coef", [P, FT])
        k.scale = k.sb("scale", [P, 1])
        k.b1e = k.sb("b1e", [HID, E_])
        k.ext_dram = nc.dram_tensor("ext_bias", (H, EXT), F32, kind="Internal")
        k.parts = [nc.dram_tensor(f"{w}_parts", (3, D, TOK), BF16, kind="Internal") for w in ("query", "key")]
        k.eo_dram = nc.dram_tensor("expert_out", (B, ES, D), F32, kind="Internal")

        k.ctxT = k.sb("ctxT", [P, KC, TOK])

        k.st = k.sb("st", [P, NT, 6])

        def stacks(scope, layer):
            k.qs = scope.enter_context(nc.sbuf_tensor(f"qs{layer}", [P, STACKS, TOK], BF16))
            k.ks = scope.enter_context(nc.sbuf_tensor(f"ks{layer}", [P, STACKS, TOK], BF16))
            if layer == 0:
                k.slab = scope.enter_context(nc.sbuf_tensor("slab", [P, STACKS, SLAB], F32))

        with nc.sbuf_tensor("v0", [P, NT, H, VW], BF16) as k.v, ExitStack() as scope:
            stacks(scope, 0)
            with nc.sbuf_tensor("hT0", [P, KC, TOK], F32) as k.hT, nc.sbuf_tensor("w0", [P, 3, KC, D], F32) as k.w0:
                with nc.sbuf_tensor("ctxin", [P, NT, D], F32) as k.ctxin:
                    load_phase(k, a)
                turn_phase(k, "t0", k.x, k.hT)
                project_phase(k, 0)
            with nc.sbuf_tensor("oraw0", [P, NT, H, VW], F32) as k.oraw:
                attention_phase(k, 0)
                residual0_phase(k)
        with nc.sbuf_tensor("w1", [P, KC, F], F32) as k.w1, nc.sbuf_tensor("w2", [P, FT, D], F32) as k.w2,                 nc.sbuf_tensor("hT1", [P, KC, TOK], F32) as k.hT:
            k.ffn_in = k.sem("ffnin")

            def load_ffn(sp):
                sp.dma_start(k.w1[:, :, :], a["L0_ffn_W1"].rearrange("(c p) f -> p c f", p=P)).then_inc(k.ffn_in, 16)
                sp.dma_start(k.w2[:, :, :], a["L0_ffn_W2"].rearrange("(c p) d -> p c d", p=P)).then_inc(k.ffn_in, 16)
            turn_phase(k, "t1", k.x, k.hT, load_ffn)
            ffn_phase(k)
        k.clear_sems()
        with nc.sbuf_tensor("v1", [P, NT, H, VW], BF16) as k.v, ExitStack() as scope:
            stacks(scope, 1)
            with nc.sbuf_tensor("hT2", [P, KC, TOK], F32) as k.hT:
                turn_phase(k, "t2", k.x, k.hT)
                project_phase(k, 1)
            with nc.sbuf_tensor("oraw1", [P, NT, H, VW], F32) as k.oraw:
                attention_phase(k, 1)
                residual1_phase(k)
        with nc.sbuf_tensor("xn", [P, NT, D], F32) as k.xn, nc.sbuf_tensor("hT3", [P, KC, TOK], F32) as k.hT, \
                nc.sbuf_tensor("mu", [P, KC, ES], F32) as k.mu, nc.sbuf_tensor("gamma", [P, D], F32) as k.gamma, \
                nc.sbuf_tensor("beta", [P, D], F32) as k.beta:
            norm_phase(k, a)
            experts_phase(k, a, out)


_OUT = ((B, S, D), "float32")


def kernel(**inputs):
    import numpy as np
    from concourse import bacc
    from concourse.bass_utils import run_bass_kernel_spmd

    nc = bacc.Bacc("TRN2", target_bir_lowering=False, num_devices=1)
    arrays, a = {}, {}
    for name, value in inputs.items():
        array = np.ascontiguousarray(value)
        arrays[f"in_{name}"] = array
        a[name] = nc.dram_tensor(f"in_{name}", array.shape, mybir.dt.from_np(array.dtype), kind="ExternalInput").ap()
    out = nc.dram_tensor("out", _OUT[0], mybir.dt.from_np(np.dtype(_OUT[1])), kind="ExternalOutput").ap()
    flamingo_kernel(nc, a, out)
    result = run_bass_kernel_spmd(nc, [arrays], core_ids=[0])
    return result.results[0]["out"]
```

```python
from contextlib import ExitStack

import concourse.bass as bass
from concourse import mybir

F32 = mybir.dt.float32
F32R = mybir.dt.float32r
BF16 = mybir.dt.bfloat16
FP16 = mybir.dt.float16
ALU = mybir.AluOpType
ACT = mybir.ActivationFunctionType
AX = mybir.AxisListType

P = 128
B, S, D = 4, 512, 256
H = 16
DH = D // H
TOK = B * S
NT = TOK // P
QT = S // P
KC = D // P
F = 1024
FT = F // P
E_, SL, HID = 16, 16, 64
ES = E_ * SL
MAXLEN = 125
REL = 2 * MAXLEN - 1
LN_EPS = 1e-5
NORM_EPS = 1e-12
PRODUCTS = ((0, 0), (0, 1), (1, 0))
TWO_PI = 6.283185307179586
SIN_SCALE = 6.283185
ROUND = 12582912.0
LOWEST = -3.0e38

TERMS = 6
KROWS = TERMS * DH
KALL = KROWS + 2
VW = 1 + 3 * DH
VLO = 1 + 2 * DH
STACKS = 4
EARLY = 2
AHEAD = 6
RING = 2 * QT
LAG = 6
SHIFT = 8.0
UNITS = H * B
BODY = STACKS * B
SLAB = S + QT * P - P
EXT = 1024


def two_pi_parts():
    import numpy as np
    hi = np.float32(6.28125)
    mid = np.float32(np.float32((TWO_PI - float(hi)) * 2 ** 20) // 1 / 2 ** 20)
    low = np.float32(TWO_PI - float(hi) - float(mid))
    return float(hi), float(mid), float(low)


class Core:

    def __init__(self, nc, ctx):
        self.nc, self.ctx = nc, ctx
        self.sems = []

    def sem(self, name):
        self.sems.append(self.nc.alloc_semaphore(name=name))
        return self.sems[-1]

    def clear_sems(self):
        with self.nc.Block() as block:
            @block.gpsimd
            def _(pool):
                for sem in self.sems[0::4]:
                    pool.sem_clear(sem)

            @block.sync
            def _(sp):
                for sem in self.sems[1::4]:
                    sp.sem_clear(sem)

            @block.vector
            def _(dve):
                for sem in self.sems[2::4]:
                    dve.sem_clear(sem)

            @block.scalar
            def _(act):
                for sem in self.sems[3::4]:
                    act.sem_clear(sem)
        for sem in self.sems:
            self.nc.release_semaphore(sem)
        self.sems = []

    def sb(self, name, shape, dt=F32):
        return self.ctx.enter_context(self.nc.sbuf_tensor(name, shape, dt))


def row(ap):
    return ap.rearrange("(a n) -> a n", a=1).to_broadcast([P, ap.shape[0]])


def tile_of(ap, t):
    return ap[:, t, :].rearrange("p a d -> p (a d)")


def column(ap):
    return ap.rearrange("(i p) -> p i", p=P)


def load_phase(k, a):
    nc = k.nc
    s = k.sem
    k.w0_in, k.ext_stored = s("ld_w0"), s("ld_extstored")
    small_in, rel_loaded, gates_loaded, theta_loaded = s("ld_small"), s("ld_rel"), s("ld_gates"), s("ld_theta")
    ctx_in, x_in = [s(f"ld_ctx{b}") for b in range(B)], [s(f"ld_x{b}") for b in range(B)]
    ctx_turned, ctx_taken = s("ld_ctxturned"), s("ld_ctxtaken")
    zeroed, diag, ident_done = s("ld_zeroed"), s("ld_diag"), s("ld_ident")
    ext_zero, ext_done = s("ld_extzero"), s("ld_extdone")
    chain, sin_in, sin_out, tanh_done = s("ld_chain"), s("ld_sinin"), s("ld_sinout"), s("ld_tanh")
    stats = s("ld_stats")
    c1, c2, c3 = two_pi_parts()
    with ExitStack() as local:
        def sb(name, shape, dt=F32):
            return local.enter_context(nc.sbuf_tensor(name, shape, dt))
        rel = sb("rel", [H, REL])
        ext = sb("ext", [H, EXT])
        th = sb("th", [P, FT])
        tb1 = sb("tb1", [P, FT])
        wr = sb("wr", [P, FT])
        wi = sb("wi", [P, FT])
        turns = sb("turns", [P, FT])
        whole = sb("whole", [P, FT])
        rem = [sb(f"rem{i}", [P, FT]) for i in range(3)]
        quarter = sb("quarter", [P, FT])
        sc = sb("sc", [P, 2, FT])
        half = sb("halfs", [P, 2, FT])
        prod = sb("prod", [P, 3, FT])
        graw = sb("graw", [P, 4])
        antif = sb("antif", [P, P])
        cbank = [local.enter_context(nc.psum_tensor(f"cbank{i}", [P, S], F32)) for i in range(4)]
        SMALL = 16 * 7
        with nc.Block() as block:
            @block.sync
            def _(sp):
                sp.dma_start(rel[:, :], a["L0_xattn_rel_emb"]).then_inc(rel_loaded, 16)
                for b in range(B):
                    sp.dma_start(k.ctxin[:, QT * b:QT * b + QT, :],
                                 a["ctx_1024"][b].rearrange("(t p) d -> p t d", p=P)).then_inc(ctx_in[b], 16)
                for b in range(B):
                    sp.dma_start(k.x[:, QT * b:QT * b + QT, :],
                                 a["x"][b].rearrange("(t p) d -> p t d", p=P)).then_inc(x_in[b], 16)
                with nc.allow_non_contiguous_dma(reason="small bias vectors, one number a partition"):
                    for layer in range(2):
                        for n, w in enumerate(("bq", "bk")):
                            sp.dma_start(k.bqk[:, layer, n, :], column(a[f"L{layer}_xattn_{w}"])).then_inc(small_in, 16)
                        sp.dma_start(k.bvb[:, layer, :], row(a[f"L{layer}_xattn_bv"])).then_inc(small_in, 16)
                    sp.dma_start(k.scale[:, :], row(a["L1_ffn_scale"])).then_inc(small_in, 16)
                for n, w in enumerate(("Wq", "Wk", "Wv")):
                    sp.dma_start(k.w0[:, n], a["L0_xattn_" + w].rearrange("(c p) o -> p c o", p=P))\
                        .then_inc(k.w0_in, 16)
                sp.wait_ge(ext_done, 6)
                sp.dma_start(k.ext_dram.ap(), ext[:, :]).then_inc(k.ext_stored, 16)
                sp.wait_ge(k.ext_stored, 16)

            @block.scalar
            def _(act):
                with nc.allow_non_contiguous_dma(reason="small bias vectors, one number a partition"):
                    act.dma_start(graw[:, 0:2], row(a["g_xattn"])).then_inc(gates_loaded, 16)
                    act.dma_start(graw[:, 2:4], row(a["g_ffn"])).then_inc(gates_loaded, 16)
                    act.dma_start(th[:, :], column(a["L0_ffn_quantum_phases"])).then_inc(theta_loaded, 16)
                    act.dma_start(wr[:, :], column(a["L0_ffn_quantum_weights_real"])).then_inc(theta_loaded, 16)
                    act.dma_start(wi[:, :], column(a["L0_ffn_quantum_weights_imag"])).then_inc(theta_loaded, 16)
                    act.dma_start(k.b1c[:, :], column(a["L0_ffn_b1"])).then_inc(theta_loaded, 16)
                def take_ctx(b):
                    for c in range(KC):
                        act.wait_ge(ctx_turned, b * KC + c + 1)
                        act.activation(k.ctxT[:, c, b * S:b * S + S], cbank[b % 2 * KC + c][:, :], ACT.Copy)\
                            .then_inc(ctx_taken, 1)

                for b in range(B):
                    take_ctx(b)
                act.wait_ge(gates_loaded, 32)
                act.activation(k.gate[:, :], graw[:, :], ACT.Tanh).then_inc(tanh_done, 1)
                act.wait_ge(sin_in, 1)
                act.activation(sc[:, 0, :], half[:, 0, :], ACT.Sin, scale=SIN_SCALE).then_inc(sin_out, 1)
                act.activation(sc[:, 1, :], half[:, 1, :], ACT.Sin, scale=SIN_SCALE).then_inc(sin_out, 1)

            @block.gpsimd
            def _(pool):
                pool.memset(k.ident[:, :], 0.0).then_inc(zeroed, 1)
                pool.memset(antif[:, :], 0.0).then_inc(zeroed, 1)
                pool.memset(k.ones[:, :], 1.0).then_inc(zeroed, 1)
                pool.wait_ge(zeroed, 3)
                pool.affine_select(out=k.ident[:, :], in_=k.ident[:, :], compare_op=ALU.not_equal, fill=1.0,
                                   base=0, pattern=[[-1, P]], channel_multiplier=1).then_inc(diag, 1)
                pool.affine_select(out=antif[:, :], in_=antif[:, :], compare_op=ALU.not_equal, fill=1.0,
                                   base=1 - P, pattern=[[1, P]], channel_multiplier=1).then_inc(diag, 1)
                pool.wait_ge(diag, 2)
                pool.tensor_scalar(k.anti[:, :], antif[:, :], 1.0, 0.0, ALU.mult, ALU.add).then_inc(ident_done, 1)
                pool.tensor_scalar(k.identb[:, :], k.ident[:, :], 1.0, 0.0, ALU.mult, ALU.add).then_inc(ident_done, 1)
                pool.wait_ge(ident_done, 2)

            @block.tensor
            def _(pe):
                pe.wait_ge(diag, 2)
                for b in range(B):
                    pe.wait_ge(ctx_in[b], 16)
                    if b >= 2:
                        pe.wait_ge(ctx_taken, (b - 1) * KC)
                    for c in range(KC):
                        for j in range(QT):
                            last = pe.transpose(cbank[b % 2 * KC + c][:, j * P:j * P + P],
                                                k.ctxin[:, b * QT + j, c * P:c * P + P], k.ident[:, :])
                        last.then_inc(ctx_turned, 1)

            @block.vector
            def _(dve):
                step = [0]

                def then(ins):
                    step[0] += 1
                    ins.then_inc(chain, 1)
                    dve.wait_ge(chain, step[0])

                dve.memset(ext[:, :], 0.0).then_inc(ext_zero, 1)
                dve.wait_ge(ext_zero, 1)
                dve.wait_ge(rel_loaded, 16)
                low = S - 1 - (MAXLEN - 1) - REL
                dve.tensor_scalar(ext[:, 0:low], ext[:, 0:low], rel[:, 0:1], None, ALU.add).then_inc(ext_done, 1)
                dve.tensor_copy(ext[:, low:low + REL], rel[:, :]).then_inc(ext_done, 1)
                dve.tensor_copy(ext[:, low + REL:low + 2 * REL], rel[:, :]).then_inc(ext_done, 1)
                dve.tensor_scalar(ext[:, low + 2 * REL:EXT - 1], ext[:, low + 2 * REL:EXT - 1],
                                  rel[:, REL - 1:REL], None, ALU.add).then_inc(ext_done, 1)
                dve.memset(ext[:, EXT - 1:EXT], 0.0).then_inc(ext_done, 1)
                dve.wait_ge(ext_done, 5)
                dve.tensor_scalar(ext[:, :], ext[:, :], rel[:, REL - 1:REL], None, ALU.subtract).then_inc(ext_done, 1)
                for b in range(B - 1):
                    dve.wait_ge(x_in[b], 16)
                    for t in range(b * QT, b * QT + QT):
                        dve.bn_stats(k.st[:, t, :], k.x[:, t, :]).then_inc(stats, 1)
                dve.wait_ge(theta_loaded, 64)
                then(dve.tensor_scalar(turns[:, :], th[:, :], 1.0 / TWO_PI, None, ALU.mult))
                then(dve.tensor_scalar(whole[:, :], turns[:, :], ROUND, ROUND, ALU.add, ALU.subtract))
                then(dve.scalar_tensor_tensor(out=rem[0][:, :], in0=whole[:, :], scalar=-c1, in1=th[:, :],
                                              op0=ALU.mult, op1=ALU.add))
                then(dve.scalar_tensor_tensor(out=rem[1][:, :], in0=whole[:, :], scalar=-c2, in1=rem[0][:, :],
                                              op0=ALU.mult, op1=ALU.add))
                then(dve.scalar_tensor_tensor(out=rem[2][:, :], in0=whole[:, :], scalar=-c3, in1=rem[1][:, :],
                                              op0=ALU.mult, op1=ALU.add))
                then(dve.tensor_scalar(half[:, 0, :], rem[2][:, :], 1.0 / TWO_PI, None, ALU.mult))
                then(dve.tensor_scalar(quarter[:, :], half[:, 0, :], 0.25, None, ALU.add))
                then(dve.tensor_scalar(prod[:, 0, :], quarter[:, :], ROUND, ROUND, ALU.add, ALU.subtract))
                then(dve.tensor_tensor(half[:, 1, :], quarter[:, :], prod[:, 0, :], ALU.subtract))
                then(dve.tensor_scalar(half[:, :, :], half[:, :, :], 0.5, -0.5, ALU.min, ALU.max))
                then(dve.tensor_scalar(tb1[:, :], k.b1c[:, :], 0.1 / TWO_PI, None, ALU.mult))
                dve.tensor_tensor(k.phase[:, :], tb1[:, :], half[:, 0, :], ALU.add).then_inc(sin_in, 1)
                for b in range(B - 1, B):
                    dve.wait_ge(x_in[b], 16)
                    for t in range(b * QT, b * QT + QT):
                        dve.bn_stats(k.st[:, t, :], k.x[:, t, :]).then_inc(stats, 1)
                dve.wait_ge(sin_out, 2)
                then(dve.tensor_tensor(prod[:, 0, :], sc[:, 1, :], wr[:, :], ALU.mult))
                then(dve.tensor_tensor(prod[:, 1, :], sc[:, 0, :], wi[:, :], ALU.mult))
                then(dve.tensor_tensor(prod[:, 2, :], prod[:, 0, :], prod[:, 1, :], ALU.add))
                then(dve.scalar_tensor_tensor(out=k.coef[:, :], in0=prod[:, 2, :], scalar=0.1, in1=wi[:, :],
                                              op0=ALU.mult, op1=ALU.mult))
                dve.wait_ge(small_in, SMALL)
                then(dve.tensor_scalar(k.bqk[:, :, 0, :], k.bqk[:, :, 0, :], DH ** -0.5, None, ALU.mult))


def turn_phase(k, name, src, dst, stacks=False, ffn=None):
    nc = k.nc
    s = lambda n: k.sem(f"{name}_{n}")
    aggr, eps_done, sd_done, rstd_done, normed, turned, taken, ones_done = map(
        s, ("aggr", "eps", "sd", "rstd", "normed", "turned", "taken", "ones"))
    low_done, w_high, w_low = map(s, ("low", "whigh", "wlow"))
    w_in = [s("w1"), s("w2")]
    AHEAD_BANKS = 2 * KC
    with ExitStack() as local:
        def sb(n, shape, dt=F32):
            return local.enter_context(nc.sbuf_tensor(f"{name}_{n}", shape, dt))
        mv = sb("mv", [P, NT, 2])
        var = sb("var", [P, NT])
        sd = sb("sd", [P, NT])
        rstd = sb("rstd", [P, NT])
        xn = sb("xn", [P, 2, QT, D])
        bank = [[local.enter_context(nc.psum_tensor(f"{name}_bank{e}{c}", [P, S], F32)) for c in range(KC)]
                for e in range(2)]
        with nc.Block() as block:
            @block.sync
            def _(sp):
                if ffn:
                    sp.dma_start(k.w1[:, 0], ffn["L0_ffn_W1"].rearrange("(c p) f -> p c f", p=P)).then_inc(w_in[0], 16)
                    sp.dma_start(k.w2[:, 0], ffn["L0_ffn_W2"].rearrange("(c p) d -> p c d", p=P)).then_inc(w_in[1], 16)

            @block.gpsimd
            def _(pool):
                if stacks:
                    pool.memset(k.ks[KROWS:KALL, :, :], 1.0).then_inc(ones_done, 1)
                if ffn:
                    pool.wait_ge(w_high, 1)
                    pool.tensor_tensor(k.w1p[:, 1], k.w1[:, 0], k.w1p[:, 0], ALU.subtract).then_inc(w_low, 1)
                    pool.wait_ge(w_in[1], 16)
                    pool.tensor_scalar(k.w2p[:, 0], k.w2[:, 0], 1.0, 0.0, ALU.mult, ALU.add).then_inc(w_high, 1)
                    pool.wait_ge(w_high, 2)
                    pool.tensor_tensor(k.w2p[:, 1], k.w2[:, 0], k.w2p[:, 0], ALU.subtract).then_inc(w_low, 1)

            @block.vector
            def _(dve):
                for t in range(NT):
                    dve.bn_aggr(mv[:, t, :], k.st[:, t, :]).then_inc(aggr, 1)
                dve.wait_ge(aggr, NT)
                dve.tensor_scalar(var[:, :], mv[:, :, 1], LN_EPS, None, ALU.add).then_inc(eps_done, 1)
                dve.wait_ge(sd_done, 1)
                dve.reciprocal(rstd[:, :], sd[:, :]).then_inc(rstd_done, 1)
                dve.wait_ge(rstd_done, 1)
                with dve.Fori(0, B // 2) as i:
                    for e in range(2):
                        dve.wait_ge(turned, i * 2 * KC + e * KC + KC)
                        for j in range(QT):
                            t = bass.ds(i * 2 * QT + e * QT + j, 1)
                            dve.tensor_scalar(xn[:, e, j, :], tile_of(src, t), mv[:, t, 0], rstd[:, t],
                                              ALU.subtract, ALU.mult).then_inc(normed, 1)
                    if ffn:
                        for e in range(2):
                            for c in range(KC):
                                dve.wait_ge(taken, i * 2 * KC + e * KC + c + 1 + AHEAD_BANKS)
                                at = bass.ds(i * 2 * S + e * S, S)
                                dve.tensor_tensor(dst[:, 1, c, at], bank[e][c][:, :], dst[:, 0, c, at], ALU.subtract)\
                                    .then_inc(low_done, 1)

            @block.scalar
            def _(act):
                act.sem_inc(taken, AHEAD_BANKS)
                act.sem_inc(low_done, AHEAD_BANKS)
                act.wait_ge(eps_done, 1)
                act.activation(sd[:, :], var[:, :], ACT.Sqrt).then_inc(sd_done, 1)
                if ffn:
                    act.wait_ge(w_in[0], 16)
                    act.activation(k.w1p[:, 0], k.w1[:, 0], ACT.Copy).then_inc(w_high, 1)
                with act.Fori(0, B // 2) as i:
                    for e in range(2):
                        for c in range(KC):
                            act.wait_ge(turned, i * 2 * KC + e * KC + c + 1 + AHEAD_BANKS)
                            at = bass.ds(i * 2 * S + e * S, S)
                            act.activation(dst[:, 0, c, at] if ffn else dst[:, c, at], bank[e][c][:, :],
                                           ACT.Copy).then_inc(taken, 1)

            @block.tensor
            def _(pe):
                pe.sem_inc(turned, AHEAD_BANKS)
                with pe.Fori(0, B // 2) as i:
                    for e in range(2):
                        pe.wait_ge(normed, i * 2 * QT + e * QT + QT)
                        pe.wait_ge(low_done if ffn else taken, i * 2 * KC + e * KC + KC)
                        for c in range(KC):
                            for j in range(QT):
                                last = pe.transpose(bank[e][c][:, j * P:j * P + P],
                                                    xn[:, e, j, c * P:c * P + P], k.ident[:, :])
                            last.then_inc(turned, 1)


def project_phase(k, layer):
    nc = k.nc
    s = lambda n: k.sem(f"pr{layer}_{n}")
    made, cut_high, rest_done, mid_done, low_done = map(s, ("made", "cuthigh", "rest", "mid", "low"))
    stored = [s(f"stored{u}") for u in range(2 * KC)]
    v_made, v_sum, v_high, v_rest, v_mid, v_low, v_ones = map(
        s, ("vmade", "vsum", "vhigh", "vrest", "vmid", "vlow", "vones"))
    bo_added = s("boadded")
    k.stack_in = [s(f"stack{i}") for i in range(STACKS)]
    wt = [k.w0[:, n] for n in range(3)] if layer == 0 else [k.wt1[:, n] for n in range(3)]
    scale = (DH ** -0.5, 1.0)
    moving = (k.hT, k.ctxT)
    RING = 2 * KC
    VBUF = 4
    with ExitStack() as local:
        def sb(n, shape, dt=F32):
            return local.enter_context(nc.sbuf_tensor(f"pr{layer}_{n}", shape, dt))
        full = sb("full", [P, RING, S])
        rest = sb("rest", [P, RING, S])
        part = sb("part", [P, RING, 3, S], BF16)
        vfull = sb("vfull", [P, VBUF, D])
        vrest = sb("vrest", [P, VBUF, D])
        bank = [local.enter_context(nc.psum_tensor(f"pr{layer}_bank{i}", [P, S], F32)) for i in range(RING)]
        vbank = [local.enter_context(nc.psum_tensor(f"pr{layer}_vbank{i}", [P, D], F32)) for i in range(VBUF)]
        units = [(w, c) for w in range(2) for c in range(KC)]
        heads = lambda ap: ap.rearrange("p (h d) -> p h d", h=H)
        with nc.Block() as block:
            @block.tensor
            def _(pe):
                if layer == 0:
                    pe.wait_ge(k.w0_in, 48)
                with pe.Fori(0, B) as b:
                    for u, (w, c) in enumerate(units):
                        pe.wait_ge(cut_high, b * RING + u + 1)
                        for kc in range(KC):
                            last = pe.matmul(bank[u][:, :], wt[w][:, kc, c * P:c * P + P],
                                             moving[w][:, kc, bass.ds(b * S, S)], start=kc == 0, stop=kc == KC - 1)
                        last.then_inc(made, 1)
                for t in range(NT):
                    if t >= VBUF:
                        pe.wait_ge(v_sum, t - VBUF + 1)
                    for kc in range(KC):
                        last = pe.matmul(vbank[t % VBUF][:, :], k.ctxT[:, kc, t * P:t * P + P], wt[2][:, kc, :],
                                         start=kc == 0, stop=kc == KC - 1)
                    last.then_inc(v_made, 1)

            @block.scalar
            def _(act):
                act.sem_inc(cut_high, RING)
                with act.Fori(0, B) as b:
                    for u, (w, c) in enumerate(units):
                        act.wait_ge(made, b * RING + u + 1)
                        act.wait_ge(low_done, b * RING + u + 1)
                        act.wait_ge(stored[u], b * 16 + 16)
                        bias = k.bqk[:, layer, w, c:c + 1]
                        act.activation(full[:, u, :], bank[u][:, :], ACT.Identity, bias=bias, scale=scale[w])
                        act.activation(part[:, u, 0, :], bank[u][:, :], ACT.Identity, bias=bias,
                                       scale=scale[w]).then_inc(cut_high, 1)
                for t in range(NT + 1):
                    if t < NT:
                        act.wait_ge(v_sum, t + 1)
                        act.activation(k.v[:, t, :, 1:1 + DH], heads(vfull[:, t % VBUF, :]), ACT.Copy)\
                            .then_inc(v_high, 1)
                    if t >= 1:
                        u = t - 1
                        act.wait_ge(v_rest, u + 1)
                        act.activation(k.v[:, u, :, 1 + DH:1 + 2 * DH], heads(vrest[:, u % VBUF, :]), ACT.Copy)\
                            .then_inc(v_mid, 1)

            @block.vector
            def _(dve):
                dve.memset(k.v[:, :, :, 0:1], 1.0).then_inc(v_ones, 1)
                with dve.Fori(0, B) as b:
                    for u in range(RING):
                        at = b * RING + u + 1
                        dve.wait_ge(cut_high, at + RING)
                        dve.tensor_tensor(rest[:, u, :], full[:, u, :], part[:, u, 0, :], ALU.subtract)\
                            .then_inc(rest_done, 1)
                        dve.wait_ge(rest_done, at)
                        dve.tensor_copy(part[:, u, 1, :], rest[:, u, :]).then_inc(mid_done, 1)
                for t in range(NT + 1):
                    if t < NT:
                        dve.wait_ge(v_made, t + 1)
                        dve.tensor_tensor(vfull[:, t % VBUF, :], vbank[t % VBUF][:, :], k.bvb[:, layer, :], ALU.add)\
                            .then_inc(v_sum, 1)
                    if t >= 1:
                        u = t - 1
                        dve.wait_ge(v_high, u + 1)
                        if u >= VBUF:
                            dve.wait_ge(v_low, u - VBUF + 1)
                        dve.tensor_tensor(heads(vrest[:, u % VBUF, :]), heads(vfull[:, u % VBUF, :]),
                                          k.v[:, u, :, 1:1 + DH], ALU.subtract).then_inc(v_rest, 1)

            @block.gpsimd
            def _(pool):
                pool.sem_inc(low_done, RING)
                with pool.Fori(0, B) as b:
                    for u in range(RING):
                        pool.wait_ge(mid_done, b * RING + u + 1)
                        pool.tensor_tensor(part[:, u, 2, :], rest[:, u, :], part[:, u, 1, :], ALU.subtract)\
                            .then_inc(low_done, 1)
                        if layer == 1:
                            xt = tile_of(k.x, bass.ds(b * QT + u, 1))
                            pool.tensor_tensor(xt, xt, k.bob[:, :], ALU.add).then_inc(bo_added, 1)
                for t in range(NT):
                    pool.wait_ge(v_mid, t + 1)
                    pool.tensor_tensor(k.v[:, t, :, 1 + 2 * DH:VW], heads(vrest[:, t % VBUF, :]),
                                       k.v[:, t, :, 1 + DH:1 + 2 * DH], ALU.subtract).then_inc(v_low, 1)

            @block.sync
            def _(sp):
                for u in range(RING):
                    sp.sem_inc(stored[u], 16)
                with sp.Fori(0, B) as b:
                    for u, (w, c) in enumerate(units):
                        sp.wait_ge(low_done, b * RING + u + 1 + RING)
                        sp.dma_start(k.parts[w].ap()[:, c * P:c * P + P, bass.ds(b * S, S)].rearrange("n p t -> p n t"),
                                     part[:, u, :, :]).then_inc(stored[u], 16)
                for u in range(RING):
                    sp.wait_ge(stored[u], 16 * (B + 1))
                for head in range(EARLY):
                    load_stacks(k, sp, layer, head, head)


def load_stacks(k, sp, layer, head, buf):
    h = bass.ds(head * DH, DH)
    qp, kp = (k.parts[w].ap() for w in range(2))
    for dst, src in ((k.qs[0:3 * DH], qp[0:3, h, :]), (k.qs[3 * DH:5 * DH], qp[0:2, h, :]),
                     (k.qs[5 * DH:6 * DH], qp[0:1, h, :]),
                     (k.ks[0:3 * DH], kp[0:1, h, :].to_broadcast([3, DH, TOK])),
                     (k.ks[3 * DH:5 * DH], kp[1:2, h, :].to_broadcast([2, DH, TOK])),
                     (k.ks[5 * DH:6 * DH], kp[2:3, h, :])):
        sp.dma_start(dst[:, buf, :], src).then_inc(k.stack_in[buf], 16)
    if layer == 0:
        r = k.ext_dram.ap()[bass.ds(head, 1), :]
        sp.dma_start(k.slab[:, buf, :], bass.AP(k.ext_dram, r.offset, [[1, P], [1, SLAB]]))\
            .then_inc(k.stack_in[buf], 16)


def attention_phase(k, layer):
    nc = k.nc
    s = lambda n: k.sem(f"at{layer}_{n}")
    biased = layer == 0
    MG = 2
    MGU = QT // MG

    def on_dve(d, kt):
        return kt == 0 or kt == 2 and d % 2 == 0

    def place(d, kt, dve):
        upto = [(u, t) for u in range(d + 1) for t in range(QT) if (u, t) <= (d, kt)]
        return sum(on_dve(*tile) == dve for tile in upto)

    max_made, max_taken, scores_made, exp_done = map(s, ("maxmade", "maxtaken", "scores", "exp"))
    lo_dve, lo_pool, pv_done, out_taken = map(s, ("lodve", "lopool", "pv", "outtaken"))
    neg_full, neg_high, neg_parts, neg_turned, neg_copied = map(
        s, ("negfull", "neghigh", "negparts", "negturned", "negcopied"))
    stack_in, qs, ks = k.stack_in, k.qs, k.ks
    neg_in = [s(f"neg{i}") for i in range(2)]
    slab_high, slab_low = s("slabhigh"), s("slablow")
    LOADS = 6 + biased
    with ExitStack() as local:
        def sb(n, shape, dt=F32):
            return local.enter_context(nc.sbuf_tensor(f"at{layer}_{n}", shape, dt))
        prob = sb("prob", [P, 2, QT, S])
        remn = sb("remn", [P, 2, QT, S], FP16)
        mx = sb("mx", [P, 2, NT])
        negf = sb("negf", [P, 2, NT])
        neg = sb("neg", [P, 2, 2, NT], BF16)
        negT = sb("negT", [2 * NT, 2, P], BF16)
        if biased:
            slab = k.slab
            tick = sb("tick", [P, 2])
            slabh = sb("slabh", [P, 2, SLAB], F32R)
            slabl = sb("slabl", [P, 2, SLAB], F32R)
        mbank = [local.enter_context(nc.psum_tensor(f"at{layer}_mb{i}", [P, MG, S], F32)) for i in range(2)]
        sbank = [local.enter_context(nc.psum_tensor(f"at{layer}_sb{i}", [P, S], F32)) for i in range(2)]
        obank = [local.enter_context(nc.psum_tensor(f"at{layer}_ob{i}", [P, S], F32)) for i in range(2)]
        high = prob[:, :, :, :].bitcast(BF16)

        def hi(buf, kt, qt):
            return high[:, buf, kt, 2 * qt * P + 1:2 * (qt + 1) * P:2]

        LAST = UNITS // BODY - 1

        def slots(eng, slot):
            for c in range(2):
                slot(0, c, True, True)
            with eng.Fori(0, LAST) as i:
                for c in range(2, BODY + 2):
                    slot(i, c, True, True)
            for c in range(2, BODY + 2):
                slot(LAST, c, c < BODY, c + AHEAD < BODY)

        def negates(i, c):
            return c % B == 2 and (not isinstance(i, int) or i * STACKS + (c + 2) // B < H)

        def slab_due(i, c):
            return biased and c % B == 0 and (i is not LAST or c + B < BODY)

        def neg_head(i, c):
            return i * STACKS + (c + 2) // B

        with nc.Block() as block:
            @block.sync
            def _(sp):
                def neg_rows(a, buf):
                    sp.wait_ge(neg_copied, a + 1)
                    for n in range(2):
                        sp.dma_start(qs[KROWS + n:KROWS + n + 1, buf, :], negT[n * NT:n * NT + NT, buf % 2, :])\
                            .then_inc(neg_in[buf % 2], 16)

                for head in range(EARLY, STACKS):
                    load_stacks(k, sp, layer, head, head)
                neg_rows(0, 0)
                with sp.Fori(0, LAST) as i:
                    for c in range(1, STACKS + 1):
                        neg_rows(i * STACKS + c, c % STACKS)
                        sp.wait_ge(scores_made, i * (STACKS * B * QT) + c * B * QT)
                        load_stacks(k, sp, layer, i * STACKS + c + STACKS - 1, (c - 1) % STACKS)
                for c in range(1, STACKS):
                    neg_rows(LAST * STACKS + c, c)

            @block.tensor
            def _(pe):
                pe.sem_inc(pv_done, RING)

                def maxima(i, d, j):
                    buf, b = d // B % STACKS, d % B
                    if b == 0 and j == 0:
                        pe.wait_ge(stack_in[buf], i * (LOADS * 16) + (d // BODY + 1) * LOADS * 16)
                    g, m = divmod(j, MG)
                    if m == 0:
                        pe.wait_ge(max_taken, i * (BODY * MGU) + d * MGU + g + 1)
                    mm = pe.matmul(mbank[g % 2][:, m, :], qs[0:KROWS, buf, b * S + j * P:b * S + j * P + P],
                                   ks[0:KROWS, buf, b * S:b * S + S], start=True, stop=True)
                    if m == MG - 1:
                        mm.then_inc(max_made, 1)

                def scores(i, d, kt):
                    buf, b = d // B % STACKS, d % B
                    if b == 0 and kt == 0:
                        pe.wait_ge(neg_in[buf % 2], i * (STACKS // 2 * 32) + (d // B // 2 + 1) * 32)
                        if biased:
                            pe.wait_ge(slab_low, i * STACKS + d // B + 1)
                    pe.wait_ge(exp_done, i * (BODY * QT) + d * QT + kt + 1)
                    mm = pe.matmul(sbank[kt % 2][:, :], ks[0:KALL, buf, b * S + kt * P:b * S + kt * P + P],
                                   qs[0:KALL, buf, b * S:b * S + S], start=True, stop=True)
                    if biased:
                        x0, n = (QT - 1 - kt) * P, min(QT, kt + 2) * P
                        pe.matmul(sbank[kt % 2][:, 0:n], k.anti[:, :], slabh[:, buf % 2, x0:x0 + n],
                                  start=False, stop=True, skip_group_check=True)
                        mm = pe.matmul(sbank[kt % 2][:, 0:n], k.anti[:, :], slabl[:, buf % 2, x0:x0 + n],
                                       start=False, stop=True, skip_group_check=True)
                    mm.then_inc(scores_made, 1)

                def values(i, d, kt):
                    buf, b = d % 2, d % B
                    if on_dve(d, kt):
                        pe.wait_ge(lo_dve, i * place(BODY - 1, QT - 1, True) + place(d, kt, True))
                    else:
                        pe.wait_ge(lo_pool, i * place(BODY - 1, QT - 1, False) + place(d, kt, False))
                    if kt == 0:
                        pe.wait_ge(out_taken, i * BODY + d + 1)
                        if negates(i, d) or d == 0:
                            pe.wait_ge(neg_copied, i * STACKS + (d + 2) // B + 1)
                    h = bass.ds(i * STACKS + d // B, 1)
                    for qt in range(QT):
                        pe.matmul(obank[buf][:, qt * 64:qt * 64 + VW], hi(buf, kt, qt), k.v[:, b * QT + kt, h, :],
                                  start=kt == 0 and qt == 0, stop=False, skip_group_check=True)
                        mm = pe.matmul(obank[buf][:, qt * 64:qt * 64 + VLO], remn[:, buf, kt, qt * P:qt * P + P],
                                       k.v[:, b * QT + kt, h, 0:VLO], start=False, stop=kt == QT - 1,
                                       skip_group_check=True)
                    mm.then_inc(pv_done, 1)

                def turn_neg(a, buf):
                    pe.wait_ge(neg_parts, a + 1)
                    pe.transpose(obank[0][:, :].bitcast(BF16)[0:2 * NT, S:S + P],
                                 neg[:, buf, :, :].rearrange("p n t -> p (n t)"), k.identb[:, :])\
                        .then_inc(neg_turned, 1)

                for d in range(AHEAD):
                    for j in range(QT):
                        maxima(0, d, j)
                    if d == B:
                        turn_neg(0, 0)

                def slot(i, c, now, ahead):
                    for j in range(QT):
                        if now:
                            scores(i, c, j)
                        if ahead:
                            maxima(i, c + AHEAD, j)
                        d, kt = divmod(c * QT + j - LAG, QT)
                        if 0 <= d < BODY or c >= BODY and now:
                            values(i, d, kt)
                    if negates(i, c):
                        pe.wait_ge(out_taken, i * BODY + c + 1)
                        turn_neg(neg_head(i, c), (c + 2) // B % 2)
                slots(pe, slot)

            @block.scalar
            def _(act):
                act.sem_inc(exp_done, 2)
                act.sem_inc(out_taken, 2)

                def exp(i, d, kt):
                    act.wait_ge(pv_done, i * (BODY * QT) + d * QT + kt + 1)
                    act.wait_ge(scores_made, i * (BODY * QT) + d * QT + kt + 1)
                    act.activation(prob[:, d % 2, kt, :], sbank[kt % 2][:, :], ACT.Exp).then_inc(exp_done, 1)

                def take_out(i, d):
                    act.wait_ge(pv_done, i * (BODY * QT) + (d + 1) * QT + RING)
                    b = d % B
                    act.activation(k.oraw[:, b * QT:b * QT + QT, bass.ds(i * STACKS + d // B, 1), :]
                                   .rearrange("p t h w -> p t (h w)"),
                                   obank[d % 2][:, 0:QT * 64].rearrange("p (t w) -> p t w", w=64)[:, :, 0:VW],
                                   ACT.Copy).then_inc(out_taken, 1)

                def copy_neg(a, buf):
                    act.wait_ge(neg_turned, a + 1)
                    act.activation(negT[:, buf, :], obank[0][:, :].bitcast(BF16)[0:2 * NT, S:S + P],
                                   ACT.Copy).then_inc(neg_copied, 1)

                def cut_slab(i, d):
                    buf = d // B % STACKS
                    act.wait_ge(stack_in[buf], i * (LOADS * 16) + (d // BODY + 1) * LOADS * 16)
                    if d // B > 1:
                        act.wait_ge(scores_made, i * (BODY * QT) + (d // B - 1) * B * QT)
                    act.activation(slabh[:, buf % 2, :], slab[:, buf, :], ACT.Copy).then_inc(slab_high, 1)

                if biased:
                    cut_slab(0, 0)
                copy_neg(0, 0)

                def slot(i, c, now, ahead):
                    for kt in range(QT):
                        if now:
                            exp(i, c, kt)
                        if kt == 2 and c >= 2:
                            take_out(i, c - 2)
                    if slab_due(i, c):
                        cut_slab(i, c + B)
                    if negates(i, c):
                        copy_neg(neg_head(i, c), (c + 2) // B % 2)
                slots(act, slot)

            @block.vector
            def _(dve):
                dve.sem_inc(max_taken, 2)

                def maxima(i, d, g):
                    dve.wait_ge(max_made, i * (BODY * MGU) + d * MGU + g + 1)
                    buf, t = d // B % 2, d % B * QT + g * MG
                    if biased:
                        dve.memset(tick[:, g:g + 1], 0.0)
                        for m in range(MG):
                            end = (g * MG + m) * P + S
                            last = slab[:, d // B % STACKS, end - 1:end]
                            back = bass.AP(slab, last.offset, [list(last.ap[0]), [-1, S]])
                            ins = dve.tensor_tensor_reduce(out=mbank[g % 2][:, m, :], in0=mbank[g % 2][:, m, :],
                                                           in1=back, scale=1.0, scalar=LOWEST, op0=ALU.add,
                                                           op1=ALU.max, accum_out=mx[:, buf, t + m:t + m + 1])
                        ins.then_inc(max_taken, 1)
                    else:
                        dve.tensor_reduce(mx[:, buf, t:t + MG], mbank[g % 2][:, :, :], AX.X, ALU.max)\
                            .then_inc(max_taken, 1)

                def negate(a, i, c, buf):
                    dve.wait_ge(max_taken, i * (BODY * MGU) + (c + AHEAD) * MGU + 2)
                    dve.tensor_scalar(negf[:, buf, :], mx[:, buf, :], -1.0, SHIFT, ALU.mult, ALU.add)\
                        .then_inc(neg_full, 1)
                    dve.wait_ge(neg_full, a + 1)
                    dve.tensor_copy(neg[:, buf, 0, :], negf[:, buf, :]).then_inc(neg_high, 1)
                    dve.wait_ge(neg_high, a + 1)
                    dve.tensor_tensor(neg[:, buf, 1, :], negf[:, buf, :], neg[:, buf, 0, :], ALU.subtract)\
                        .then_inc(neg_parts, 1)

                def remainder(i, d, kt):
                    dve.wait_ge(exp_done, i * (BODY * QT) + d * QT + kt + 1 + 2)
                    dve.tensor_tensor(remn[:, d % 2, kt, :], prob[:, d % 2, kt, :], high[:, d % 2, kt, 1::2],
                                      ALU.subtract).then_inc(lo_dve, 1)

                for d in range(AHEAD):
                    for g in range(MGU):
                        maxima(0, d, g)
                    if d == B - 1:
                        negate(0, 0, B - AHEAD, 0)

                def slot(i, c, now, ahead):
                    if negates(i, c):
                        negate(neg_head(i, c), i, c, (c + 2) // B % 2)
                    for g in range(MGU):
                        if ahead:
                            maxima(i, c + AHEAD, g)
                        for kt in range(g * MG, g * MG + MG):
                            if now and on_dve(c, kt):
                                remainder(i, c, kt)
                slots(dve, slot)

            @block.gpsimd
            def _(pool):
                def slab_rest(i, d):
                    buf, a = d // B % STACKS, i * STACKS + d // B
                    pool.wait_ge(slab_high, a + 1)
                    pool.tensor_tensor(slabl[:, buf % 2, :], slab[:, buf, :], slabh[:, buf % 2, :],
                                       ALU.subtract).then_inc(slab_low, 1)

                def remainders(i, d):
                    for kt in range(QT):
                        if not on_dve(d, kt):
                            pool.wait_ge(exp_done, i * (BODY * QT) + d * QT + kt + 1 + 2)
                            pool.tensor_tensor(remn[:, d % 2, kt, :], prob[:, d % 2, kt, :],
                                               high[:, d % 2, kt, 1::2], ALU.subtract).then_inc(lo_pool, 1)

                if biased:
                    slab_rest(0, 0)

                def slot(i, c, now, ahead):
                    if now:
                        remainders(i, c)
                    if slab_due(i, c):
                        slab_rest(i, c + B)
                slots(pool, slot)


PAIR = 2


class Combine:

    def __init__(self, k, name, local, gated):
        s = lambda n: k.sem(f"{name}_{n}")
        self.k, self.gated = k, gated
        self.rec_done, self.small_done, self.whole_done, self.out_done = map(s, ("rec", "small", "whole", "out"))
        sb = lambda n, shape: local.enter_context(k.nc.sbuf_tensor(f"{name}_{n}", shape, F32))
        self.small = sb("small", [P, 2, PAIR, H, DH])
        self.whole = sb("whole", [P, 3, PAIR, H, DH])
        self.out = sb("out", [P, 3, PAIR, D])
        self.rec = sb("rec", [P, NT, H])

    def part(self, n, n_of):
        return self.k.oraw[:, n * PAIR:n * PAIR + PAIR, :, 1 + n_of * DH:1 + (n_of + 1) * DH]

    def pool_steps(self, pool):
        for n in range(NT // PAIR):
            if n >= 2:
                pool.wait_ge(self.whole_done, n - 1)
            pool.tensor_tensor(self.small[:, n % 2], self.part(n, 1), self.part(n, 2), ALU.add)\
                .then_inc(self.small_done, 1)

    def reciprocals(self, dve):
        dve.reciprocal(self.rec[:, :, :], self.k.oraw[:, :, :, 0]).then_inc(self.rec_done, 1)
        dve.wait_ge(self.rec_done, 1)
        if self.gated:
            dve.tensor_scalar(self.rec[:, :, :], self.rec[:, :, :], self.k.gate[:, 0:1], None, ALU.mult)\
                .then_inc(self.rec_done, 1)
            dve.wait_ge(self.rec_done, 2)

    def dve_add(self, dve, n):
        dve.wait_ge(self.small_done, n + 1)
        if n >= 3:
            dve.wait_ge(self.out_done, n - 2)
        dve.tensor_tensor(self.whole[:, n % 3], self.part(n, 0), self.small[:, n % 2], ALU.add)\
            .then_inc(self.whole_done, 1)

    def dve_divide(self, dve, n):
        dve.wait_ge(self.whole_done, n + 1)
        rec = self.rec[:, n * PAIR:n * PAIR + PAIR, :].unsqueeze(3).to_broadcast([P, PAIR, H, DH])
        dve.tensor_tensor(self.out[:, n % 3].rearrange("p t (h d) -> p t h d", h=H), self.whole[:, n % 3],
                          rec, ALU.mult).then_inc(self.out_done, 1)


def residual0_phase(k, a):
    nc = k.nc
    added, stats = k.sem("r0_added"), k.sem("r0_stats")
    w_in, b_in, turned, taken, gated = (k.sem("r0_" + n) for n in ("w", "b", "turned", "taken", "gated"))
    with ExitStack() as local:
        wraw = local.enter_context(nc.sbuf_tensor("wraw", [P, 4, KC, D], F32))
        braw = local.enter_context(nc.sbuf_tensor("braw", [P, 2, D], F32))
        bank = [local.enter_context(nc.psum_tensor(f"r0_bank{i}", [P, 512], F32)) for i in range(4)]
        comb = Combine(k, "r0", local, True)
        with nc.Block() as block:
            @block.sync
            def _(sp):
                for n, w in enumerate(("Wq", "Wk", "Wv", "Wo")):
                    sp.dma_start(wraw[:, n], a["L1_xattn_" + w].rearrange("(c p) i -> p c i", p=P)).then_inc(w_in, 16)
                sp.dma_start(braw[:, 0, :], row(a["L0_ffn_b2"])).then_inc(b_in, 16)
                sp.dma_start(braw[:, 1, :], row(a["L1_xattn_bo"])).then_inc(b_in, 16)

            @block.tensor
            def _(pe):
                pe.wait_ge(w_in, 64)
                for n in range(4):
                    for ic in range(KC):
                        for oc in range(KC):
                            last = pe.transpose(bank[n][:, ic * D + oc * P:ic * D + oc * P + P],
                                                wraw[:, n, oc, ic * P:ic * P + P], k.ident[:, :])
                    last.then_inc(turned, 1)

            @block.scalar
            def _(act):
                for n in range(4):
                    act.wait_ge(turned, n + 1)
                    act.activation(k.wt1[:, n, :, :], bank[n][:, :].rearrange("p (c o) -> p c o", c=KC),
                                   ACT.Copy).then_inc(taken, 1)
                act.wait_ge(b_in, 32)
                act.activation(k.b2b[:, :], braw[:, 0, :], ACT.Copy, scale=k.gate[:, 2:3]).then_inc(gated, 1)
                act.activation(k.bob[:, :], braw[:, 1, :], ACT.Copy, scale=k.gate[:, 1:2]).then_inc(gated, 1)

            @block.gpsimd
            def _(pool):
                comb.pool_steps(pool)

            @block.vector
            def _(dve):
                comb.reciprocals(dve)
                STEPS = NT // PAIR
                for n in range(STEPS + 3):
                    if n < STEPS:
                        comb.dve_add(dve, n)
                    if 2 <= n <= STEPS + 1:
                        u = n - 2
                        dve.wait_ge(comb.out_done, u + 1)
                        dve.tensor_tensor(k.x[:, u * PAIR:u * PAIR + PAIR, :], comb.out[:, u % 3],
                                          k.x[:, u * PAIR:u * PAIR + PAIR, :], ALU.add).then_inc(added, 1)
                    if 1 <= n <= STEPS:
                        if n >= 4:
                            dve.wait_ge(added, n - 3)
                        comb.dve_divide(dve, n - 1)
                    if n >= 3:
                        dve.wait_ge(added, n - 2)
                        for t in range((n - 3) * PAIR, (n - 2) * PAIR):
                            dve.bn_stats(k.st[:, t, :], k.x[:, t, :]).then_inc(stats, 1)


def residual1_phase(k):
    nc = k.nc
    turned, turned_out, made, added, stats = (
        k.sem("r1_" + n) for n in ("turned", "turnedout", "made", "added", "stats"))
    STEPS = NT // PAIR
    with ExitStack() as local:
        comb = Combine(k, "r1", local, False)
        oT = local.enter_context(nc.sbuf_tensor("r1_oT", [P, 2, PAIR, KC, P], F32))
        tb = [local.enter_context(nc.psum_tensor(f"r1_tb{i}", [P, PAIR, KC, P], F32)) for i in range(2)]
        yb = [local.enter_context(nc.psum_tensor(f"r1_yb{i}", [P, PAIR, D], F32)) for i in range(2)]
        with nc.Block() as block:
            @block.vector
            def _(dve):
                comb.reciprocals(dve)
                for n in range(STEPS + 4):
                    if n < STEPS:
                        comb.dve_add(dve, n)
                    if 1 <= n <= STEPS:
                        if n >= 4:
                            dve.wait_ge(turned, n - 3)
                        comb.dve_divide(dve, n - 1)
                    if 3 <= n <= STEPS + 2:
                        u = n - 3
                        dve.wait_ge(made, u + 1)
                        xs = k.x[:, u * PAIR:u * PAIR + PAIR, :]
                        dve.scalar_tensor_tensor(out=xs, in0=yb[u % 2][:, :, :], scalar=k.gate[:, 1:2], in1=xs,
                                                 op0=ALU.mult, op1=ALU.add).then_inc(added, 1)
                    if n >= 4:
                        dve.wait_ge(added, n - 3)
                        for t in range((n - 4) * PAIR, (n - 3) * PAIR):
                            dve.bn_stats(k.st[:, t, :], k.x[:, t, :]).then_inc(stats, 1)

            @block.gpsimd
            def _(pool):
                comb.pool_steps(pool)

            @block.scalar
            def _(act):
                for n in range(STEPS):
                    act.wait_ge(turned, n + 1)
                    if n >= 2:
                        act.wait_ge(made, n - 1)
                    act.activation(oT[:, n % 2], tb[n % 2][:, :, :, :], ACT.Copy).then_inc(turned_out, 1)

            @block.tensor
            def _(pe):
                for n in range(STEPS + 1):
                    if n < STEPS:
                        pe.wait_ge(comb.out_done, n + 1)
                        if n >= 2:
                            pe.wait_ge(turned_out, n - 1)
                        for m in range(PAIR):
                            for c in range(KC):
                                last = pe.transpose(tb[n % 2][:, m, c, :], comb.out[:, n % 3, m, c * P:c * P + P],
                                                    k.ident[:, :])
                        last.then_inc(turned, 1)
                    if n >= 1:
                        u = n - 1
                        pe.wait_ge(turned_out, u + 1)
                        if u >= 2:
                            pe.wait_ge(added, u - 1)
                        for m in range(PAIR):
                            for c in range(KC):
                                last = pe.matmul(yb[u % 2][:, m, :], oT[:, u % 2, m, c, :], k.wt1[:, 3, c, :],
                                                 start=c == 0, stop=c == KC - 1)
                        last.then_inc(made, 1)


def ffn_phase(k):
    nc = k.nc
    s = lambda n: k.sem("ff_" + n)
    h_made, turns_done, whole_done, frac_done, sin_done, mixed, relu_done, low_done = map(
        s, ("hmade", "turns", "whole", "frac", "sin", "mixed", "relu", "low"))
    y_made, y_taken, b2_added, stats = map(s, ("ymade", "ytaken", "b2added", "stats"))
    HB = 4
    with ExitStack() as local:
        def sb(n, shape, dt=F32):
            return local.enter_context(nc.sbuf_tensor("ff_" + n, shape, dt))
        turns, whole, frac, sine, mix = (sb(n, [P, 2, S]) for n in ("turns", "whole", "frac", "sine", "mix"))
        hid = sb("hid", [P, HB, S])
        hidp = sb("hidp", [P, 2, HB, S], F32R)
        hb = [local.enter_context(nc.psum_tensor(f"ff_hb{i}", [P, S], F32)) for i in range(HB)]
        yb = [local.enter_context(nc.psum_tensor(f"ff_yb{i}", [P, D], F32)) for i in range(QT)]

        def slots(eng, slot, lag):
            for f in range(lag):
                slot(0, f, True)
            with eng.Fori(0, B - 1) as b:
                for f in range(lag, FT + lag):
                    slot(b, f, True)
            for f in range(lag, FT + lag):
                slot(B - 1, f, f < FT)

        with nc.Block() as block:
            @block.tensor
            def _(pe):
                pe.sem_inc(y_made, HB)

                def slot(b, f, now):
                    if now:
                        pe.wait_ge(mixed, b * FT + f + 1)
                        at = bass.ds(b * S + f // FT * S, S)
                        for n, (c, (wp, hp)) in enumerate((c, p) for c in range(KC) for p in PRODUCTS):
                            last = pe.matmul(hb[f % HB][:, :], k.w1p[:, wp, c, f % FT * P:f % FT * P + P],
                                             k.hTp[:, hp, c, at], start=n == 0, stop=n == 3 * KC - 1)
                        last.then_inc(h_made, 1)
                    u = f - HB
                    if u >= 0:
                        pe.wait_ge(low_done, b * FT + u + 1)
                        if u % FT == 0:
                            pe.wait_ge(y_taken, b * QT + u // FT * QT + 1)
                        for j in range(QT):
                            for n, (hp, wp) in enumerate(PRODUCTS):
                                last = pe.matmul(yb[j][:, :], hidp[:, hp, u % HB, j * P:j * P + P],
                                                 k.w2p[:, wp, u % FT, :], start=u % FT == 0 and n == 0,
                                                 stop=u % FT == FT - 1 and n == 2, skip_group_check=True)
                        last.then_inc(y_made, 1)
                slots(pe, slot, HB)

            @block.scalar
            def _(act):
                def slot(b, f, now):
                    if now:
                        act.wait_ge(h_made, b * FT + f + 1)
                        act.activation(turns[:, f % 2, :], hb[f % HB][:, :], ACT.Identity,
                                       bias=k.phase[:, f % FT:f % FT + 1], scale=0.1 / TWO_PI).then_inc(turns_done, 1)
                    u = f - 1
                    if u >= 0 and (now or u < FT):
                        act.wait_ge(frac_done, b * FT + u + 1)
                        act.activation(sine[:, u % 2, :], frac[:, u % 2, :], ACT.Sin, scale=SIN_SCALE)\
                            .then_inc(sin_done, 1)
                    u = f - 2
                    if u >= 0:
                        act.wait_ge(mixed, b * FT + u + 1 + HB)
                        act.wait_ge(y_made, b * FT + u + 1)
                        bias = k.b1c[:, u % FT:u % FT + 1]
                        act.activation(hid[:, u % HB, :], mix[:, u % 2, :], ACT.Relu, bias=bias)
                        act.activation(hidp[:, 0, u % HB, :], mix[:, u % 2, :], ACT.Relu, bias=bias)\
                            .then_inc(relu_done, 1)
                slots(act, slot, 2)

            @block.vector
            def _(dve):
                dve.sem_inc(mixed, HB)
                dve.sem_inc(y_taken, 1)

                def slot(b, f, now):
                    if f == FT + HB:
                        dve.wait_ge(y_made, b * FT + FT + HB)
                        dve.wait_ge(b2_added, b * QT + QT)
                        for j in range(QT):
                            xt = tile_of(k.x, bass.ds(b * QT + j, 1))
                            dve.scalar_tensor_tensor(out=xt, in0=yb[j][:, :], scalar=k.gate[:, 2:3], in1=xt,
                                                     op0=ALU.mult, op1=ALU.add).then_inc(y_taken, 1)
                    if now:
                        dve.wait_ge(turns_done, b * FT + f + 1)
                        dve.tensor_scalar(whole[:, f % 2, :], turns[:, f % 2, :], ROUND, ROUND,
                                          ALU.add, ALU.subtract).then_inc(whole_done, 1)
                        dve.wait_ge(whole_done, b * FT + f + 1)
                        dve.tensor_tensor(frac[:, f % 2, :], turns[:, f % 2, :], whole[:, f % 2, :],
                                          ALU.subtract).then_inc(frac_done, 1)
                    u = f - 1
                    if u >= 0 and (now or u < FT):
                        dve.wait_ge(sin_done, b * FT + u + 1)
                        if u >= 2:
                            dve.wait_ge(relu_done, b * FT + u - 1)
                        dve.scalar_tensor_tensor(out=mix[:, u % 2, :], in0=sine[:, u % 2, :],
                                                 scalar=k.coef[:, u % FT:u % FT + 1], in1=hb[u % HB][:, :],
                                                 op0=ALU.mult, op1=ALU.add).then_inc(mixed, 1)
                    if f == FT + HB:
                        for j in range(QT):
                            t = bass.ds(b * QT + j, 1)
                            dve.wait_ge(y_taken, b * QT + j + 2)
                            dve.bn_stats(tile_of(k.st, t), tile_of(k.x, t)).then_inc(stats, 1)
                slots(dve, slot, HB + 1)

            @block.gpsimd
            def _(pool):
                with pool.Fori(0, B) as b:
                    for f in range(FT):
                        pool.wait_ge(relu_done, b * FT + f + 1)
                        pool.tensor_tensor(hidp[:, 1, f % HB, :], hid[:, f % HB, :], hidp[:, 0, f % HB, :],
                                           ALU.subtract).then_inc(low_done, 1)
                        if f % 2:
                            xt = tile_of(k.x, bass.ds(b * QT + f // 2, 1))
                            pool.tensor_tensor(xt, xt, k.b2b[:, :], ALU.add).then_inc(b2_added, 1)


def norm_phase(k, a):
    nc = k.nc
    s = lambda n: k.sem("mn_" + n)
    chain, sqrt_in, sqrt_out, turned, taken = map(s, ("chain", "sqrtin", "sqrtout", "turned", "taken"))
    first_in, first_done, stats, scaled, xn_done, squares, unit_in, unit_done, unit_act = map(
        s, ("firstin", "first", "stats", "scaled", "xn", "squares", "unitin", "unit", "unitact"))
    mu_sq, mu_sum, w_in, low_done = s("musq"), s("musum"), s("w"), s("low")
    with ExitStack() as local:
        def sb(n, shape, dt=F32):
            return local.enter_context(nc.sbuf_tensor("mn_" + n, shape, dt))
        st = sb("st", [P, NT, 6])
        mv = sb("mv", [P, 2, NT, 2])
        var = sb("var", [P, 2, NT])
        sd = sb("sd", [P, 2, NT])
        rstd = sb("rstd", [P, 2, NT])
        shift = sb("shift", [P, NT])
        first = sb("first", [P, NT, D])
        middle = sb("middle", [P, 4, D])
        norm2 = sb("norm2", [P, NT])
        norm = sb("norm", [P, NT])
        unit = sb("unit", [P, NT])
        junk = sb("junk", [P, 2, D])
        xu = sb("xu", [P, 2, QT, D])
        sq = sb("sq", [P, KC, ES])
        munorm = sb("munorm", [P, ES])
        murec = sb("murec", [P, ES])
        mub = local.enter_context(nc.psum_tensor("mn_mub", [P, ES], F32))
        bank = [local.enter_context(nc.psum_tensor(f"mn_bank{i}", [P, S], F32)) for i in range(2 * KC)]
        with nc.Block() as block:
            @block.vector
            def _(dve):
                n = [0]

                def then(*instructions):
                    for ins in instructions:
                        n[0] += 1
                        ins.then_inc(chain, 1)
                    dve.wait_ge(chain, n[0])

                def deviations(m):
                    dve.tensor_scalar(var[:, m, :], mv[:, m, :, 1], LN_EPS, None, ALU.add).then_inc(sqrt_in, 1)
                    dve.wait_ge(sqrt_out, m + 1)
                    then(dve.reciprocal(rstd[:, m, :], sd[:, m, :]))

                def low_parts(b):
                    for c in range(KC):
                        dve.wait_ge(taken, b * KC + c + 1)
                        at = slice(b * S, b * S + S)
                        dve.tensor_tensor(k.hTp[:, 1, c, at], bank[(b % 2) * KC + c][:, :], k.hTp[:, 0, c, at],
                                          ALU.subtract).then_inc(low_done, 1)

                def unit_columns():
                    dve.wait_ge(sqrt_out, 3)
                    then(dve.tensor_scalar(munorm[:, :], munorm[:, :], NORM_EPS, None, ALU.max))
                    then(dve.reciprocal(murec[:, :], munorm[:, :]))
                    then(*[dve.tensor_tensor(k.mu[:, c, :], k.mu[:, c, :], murec[:, :], ALU.mult) for c in range(KC)])
                    then(dve.tensor_copy(k.mup[:, 0], k.mu[:, :, :]))
                    then(dve.tensor_tensor(k.mup[:, 1], k.mu[:, :, :], k.mup[:, 0], ALU.subtract))

                then(*[dve.bn_aggr(mv[:, 0, t, :], k.st[:, t, :]) for t in range(NT)])
                deviations(0)
                dve.scalar_tensor_tensor(out=shift[:, :], in0=mv[:, 0, :, 0], scalar=-1.0, in1=rstd[:, 0, :],
                                         op0=ALU.mult, op1=ALU.mult).then_inc(first_in, 1)
                dve.wait_ge(w_in, 48)
                dve.tensor_tensor(sq[:, :, :], k.mu[:, :, :], k.mu[:, :, :], ALU.mult).then_inc(mu_sq, 1)
                for t in range(NT):
                    dve.wait_ge(first_done, t + 1)
                    dve.bn_stats(st[:, t, :], first[:, t, :]).then_inc(stats, 1)
                dve.wait_ge(stats, NT)
                then(*[dve.bn_aggr(mv[:, 1, t, :], st[:, t, :]) for t in range(NT)])
                deviations(1)
                for t in range(NT + 1):
                    if t < NT:
                        if t >= 4:
                            dve.wait_ge(xn_done, t - 3)
                        dve.scalar_tensor_tensor(out=middle[:, t % 4, :], in0=first[:, t, :], scalar=mv[:, 1, t, 0:1],
                                                 in1=k.gamma[:, :], op0=ALU.subtract, op1=ALU.mult).then_inc(scaled, 1)
                    if t:
                        u = t - 1
                        dve.wait_ge(scaled, u + 1)
                        dve.scalar_tensor_tensor(out=k.xn[:, u, :], in0=middle[:, u % 4, :],
                                                 scalar=rstd[:, 1, u:u + 1], in1=k.beta[:, :],
                                                 op0=ALU.mult, op1=ALU.add).then_inc(xn_done, 1)
                dve.wait_ge(sqrt_out, 4)
                then(dve.tensor_scalar(norm[:, :], norm[:, :], NORM_EPS, None, ALU.max))
                then(dve.reciprocal(unit[:, :], norm[:, :]))
                dve.tensor_scalar(unit[:, :], unit[:, :], k.scale[:, 0:1], None, ALU.mult).then_inc(unit_in, 1)
                dve.wait_ge(unit_in, 1)
                for t in range(0, NT, 2):
                    b, j = divmod(t, QT)
                    if b >= 2 and j == 0:
                        dve.wait_ge(turned, KC * (b - 1))
                    dve.tensor_scalar(xu[:, b % 2, j, :], k.xn[:, t, :], unit[:, t:t + 1], None, ALU.mult)\
                        .then_inc(unit_done, 1)
                    if t == QT:
                        unit_columns()
                    if b >= 1 and j == 2:
                        low_parts(b - 1)
                low_parts(B - 1)

            @block.scalar
            def _(act):
                act.wait_ge(sqrt_in, 1)
                act.activation(sd[:, 0, :], var[:, 0, :], ACT.Sqrt).then_inc(sqrt_out, 1)
                act.wait_ge(first_in, 1)
                for t in range(NT):
                    act.activation(first[:, t, :], k.x[:, t, :], ACT.Identity, bias=shift[:, t:t + 1],
                                   scale=rstd[:, 0, t:t + 1]).then_inc(first_done, 1)
                act.wait_ge(sqrt_in, 2)
                act.activation(sd[:, 1, :], var[:, 1, :], ACT.Sqrt).then_inc(sqrt_out, 1)
                act.wait_ge(mu_sum, 1)
                act.activation(munorm[:, :], mub[:, :], ACT.Sqrt).then_inc(sqrt_out, 1)
                for t in range(NT):
                    act.wait_ge(xn_done, t + 1)
                    if t >= 2:
                        act.wait_ge(squares, t - 1)
                    act.activation(junk[:, t % 2, :], k.xn[:, t, :], ACT.Square, accum_out=norm2[:, t:t + 1])\
                        .then_inc(squares, 1)
                act.wait_ge(squares, NT)
                act.activation(norm[:, :], norm2[:, :], ACT.Sqrt).then_inc(sqrt_out, 1)
                act.wait_ge(unit_in, 1)
                for b in range(B + 1):
                    if b < B:
                        if b >= 2:
                            act.wait_ge(turned, KC * (b - 1))
                        for j in range(1, QT, 2):
                            t = b * QT + j
                            act.activation(xu[:, b % 2, j, :], k.xn[:, t, :], ACT.Copy, scale=unit[:, t:t + 1])\
                                .then_inc(unit_act, 1)
                    if b >= 1:
                        for c in range(KC):
                            u = b - 1
                            act.wait_ge(turned, u * KC + c + 1)
                            act.activation(k.hTp[:, 0, c, u * S:u * S + S], bank[(u % 2) * KC + c][:, :], ACT.Copy)\
                                .then_inc(taken, 1)

            @block.tensor
            def _(pe):
                pe.wait_ge(mu_sq, 1)
                for c in range(KC):
                    last = pe.matmul(mub[:, :], k.ones[:, :], sq[:, c, :], start=c == 0, stop=c == KC - 1)
                last.then_inc(mu_sum, 1)
                for b in range(B):
                    pe.wait_ge(unit_done, (b + 1) * QT // 2)
                    pe.wait_ge(unit_act, (b + 1) * QT // 2)
                    if b >= 2:
                        pe.wait_ge(low_done, (b - 1) * KC)
                    for c in range(KC):
                        for j in range(QT):
                            last = pe.transpose(bank[(b % 2) * KC + c][:, j * P:j * P + P],
                                                xu[:, b % 2, j, c * P:c * P + P], k.ident[:, :])
                        last.then_inc(turned, 1)

            @block.sync
            def _(sp):
                sp.dma_start(k.mu[:, :, :], a["L1_ffn_mu"].rearrange("(c p) e s -> p c (e s)", p=P)).then_inc(w_in, 16)
                sp.dma_start(k.gamma[:, :], row(a["L1_ffn_ln_gamma"])).then_inc(w_in, 16)
                sp.dma_start(k.beta[:, :], row(a["L1_ffn_ln_beta"])).then_inc(w_in, 16)


def experts_phase(k, a, out):
    nc = k.nc
    s = lambda n: k.sem("me_" + n)
    EC = ES // P
    EH = E_ // EC
    lg_made, mx_done, exp_done = map(s, ("logits", "mx", "exp"))
    disp_turned, disp_out, comb_turned, comb_out = map(s, ("dispT", "dispout", "combT", "combout"))
    slot_made, slot_norm, slotT_made, slotT_out = map(s, ("slot", "slotnorm", "slotT", "slotTout"))
    rec_done, sums_done = map(s, ("rec", "sums"))
    hid_made, gelu_done, out_made, out_copied, back = map(s, ("hid", "gelu", "out", "outcopied", "back"))
    stored = [s(f"stored{c}") for c in range(EC)]
    w_in, zeroed, comb_made, added, out_stored = map(s, ("w", "zeroed", "combmade", "added", "outstored"))
    with ExitStack() as local:
        def sb(n, shape, dt=F32):
            return local.enter_context(nc.sbuf_tensor("me_" + n, shape, dt))

        def ps(n, shape, dt=F32):
            return local.enter_context(nc.psum_tensor("me_" + n, shape, dt))
        ew1 = sb("ew1", [P, KC, EH, EC, HID])
        ew2 = sb("ew2", [P, EH, D])
        eb1 = sb("eb1", [P, EH])
        eb2 = sb("eb2", [P, EH, D])
        mxs = sb("mxs", [P, B, EC])
        mxt = sb("mxt", [P, B, QT])
        sums = sb("sums", [P, B, EC])
        sumt = sb("sumt", [P, B, QT])
        recs = sb("recs", [P, B, EC])
        rect = sb("rect", [P, B, QT])
        scale = sb("scale", [P, B, QT])
        eslot = sb("eslot", [P, EC, S])
        etok = sb("etok", [P, 2, QT, ES])
        disp = sb("disp", [P, QT, ES])
        comb = sb("comb", [P, B, EC, S])
        slot = sb("slot", [P, EC, D])
        slotT = sb("slotT", [P, KC, EH, EC, B, SL])
        hid = sb("hid", [P, EH, P])
        eo = sb("eo", [P, EH, D])
        so = sb("so", [P, EC, B, D])
        lgs = ps("lgs", [P, EC, S])
        lgt = ps("lgt", [P, QT, ES])
        tr = ps("tr", [P, 2, 512])
        acc = ps("acc", [P, EC, D])
        tp = ps("tp", [P, KC, EC, P])
        hb = [tr[:, i, :] for i in range(2)]
        ob = [lgs[:, 0, :], lgs[:, 1, :]]
        cb = [tr[:, 0, :], tr[:, 1, :], lgt[:, 0:2, :].rearrange("p a s -> p (a s)"),
              lgt[:, 2:4, :].rearrange("p a s -> p (a s)")]

        with nc.Block() as block:
            @block.tensor
            def _(pe):
                steps = [(c, parts) for c in range(KC) for parts in PRODUCTS]

                def logits(b):
                    if b:
                        pe.wait_ge(exp_done, 2 * b - 1)
                    for e in range(EC):
                        for n, (c, (wp, hp)) in enumerate(steps):
                            last = pe.matmul(lgs[:, e, :], k.mup[:, wp, c, e * P:e * P + P],
                                             k.hTp[:, hp, c, b * S:b * S + S], start=n == 0, stop=n == len(steps) - 1)
                    last.then_inc(lg_made, 1)
                    if b:
                        pe.wait_ge(exp_done, 2 * b)
                    for j in range(QT):
                        t = b * QT + j
                        for n, (c, (wp, hp)) in enumerate(steps):
                            last = pe.matmul(lgt[:, j, :], k.hTp[:, hp, c, t * P:t * P + P], k.mup[:, wp, c, :],
                                             start=n == 0, stop=n == len(steps) - 1)
                    last.then_inc(lg_made, 1)

                def turn_slots(b):
                    pe.wait_ge(slot_norm, (b + 1) * EC)
                    if b:
                        pe.wait_ge(slotT_out, b)
                    for e in range(EC):
                        for c in range(KC):
                            last = pe.transpose(tp[:, c, e, :], slot[:, e, c * P:c * P + P], k.ident[:, :])
                    last.then_inc(slotT_made, 1)

                logits(0)
                for b in range(B):
                    pe.wait_ge(exp_done, 2 * b + 1)
                    if b:
                        pe.wait_ge(comb_out, b)
                    for j in range(QT):
                        for e in range(EC):
                            last = pe.transpose(tr[:, j // 2, j % 2 * ES + e * P:j % 2 * ES + e * P + P],
                                                eslot[:, e, j * P:j * P + P], k.ident[:, :])
                    last.then_inc(disp_turned, 1)
                    if b + 1 < B:
                        logits(b + 1)
                    if b:
                        turn_slots(b - 1)
                    pe.wait_ge(exp_done, 2 * b + 2)
                    pe.wait_ge(disp_out, b + 1)
                    for e in range(EC):
                        for j in range(QT):
                            last = pe.transpose(tr[:, e, j * P:j * P + P], etok[:, b % 2, j, e * P:e * P + P],
                                                k.ident[:, :])
                    last.then_inc(comb_turned, 1)
                    if b:
                        pe.wait_ge(slot_norm, b * EC)
                    for e in range(EC):
                        for j in range(QT):
                            last = pe.matmul(acc[:, e, :], disp[:, j, e * P:e * P + P], k.xn[:, b * QT + j, :],
                                             start=j == 0, stop=j == QT - 1)
                        last.then_inc(slot_made, 1)
                turn_slots(B - 1)
                pe.wait_ge(slotT_out, B)
                pe.wait_ge(comb_out, B)
                pe.wait_ge(w_in, 16 * (KC * EC + 3 * EC))
                pe.wait_ge(zeroed, 1)
                for u in range(EH + 2):
                    if u < EH:
                        if u >= 2:
                            pe.wait_ge(gelu_done, u - 1)
                        for c in range(KC):
                            last = pe.matmul(hb[u % 2][:, 0:P], ew1[:, c, u].rearrange("p t h -> p (t h)"),
                                             slotT[:, c, u].rearrange("p t b s -> p (t b s)"),
                                             start=c == 0, stop=c == KC - 1)
                        last.then_inc(hid_made, 1)
                    if u >= 2:
                        v = u - 2
                        pe.wait_ge(gelu_done, v + 1)
                        if v >= 2:
                            pe.wait_ge(out_copied, v - 1)
                        pe.matmul(ob[v % 2][:, 0:D], hid[:, v, :], ew2[:, v, :], start=True, stop=True)\
                            .then_inc(out_made, 1)
                pe.wait_ge(back, 16 * EC)
                for t in range(NT):
                    b, j = divmod(t, QT)
                    if t >= 4:
                        pe.wait_ge(added, t - 3)
                    for e in range(EC):
                        last = pe.matmul(cb[t % 4][:, 0:D], comb[:, b, e, j * P:j * P + P], so[:, e, b, :],
                                         start=e == 0, stop=e == EC - 1)
                    last.then_inc(comb_made, 1)

            @block.vector
            def _(dve):
                def maxima(b):
                    dve.wait_ge(lg_made, 2 * b + 1)
                    dve.tensor_reduce(mxs[:, b, :], lgs[:, :, :], AX.X, ALU.max, negate=True).then_inc(mx_done, 1)
                    dve.wait_ge(lg_made, 2 * b + 2)
                    dve.tensor_reduce(mxt[:, b, :], lgt[:, :, :], AX.X, ALU.max, negate=True).then_inc(mx_done, 1)
                maxima(0)
                for b in range(B):
                    dve.wait_ge(disp_turned, b + 1)
                    if b:
                        dve.wait_ge(slot_made, b * EC)
                    dve.tensor_copy(disp[:, :, :].rearrange("p j s -> p (j s)"),
                                    tr[:, :, :].rearrange("p a s -> p (a s)")).then_inc(disp_out, 1)
                    dve.reciprocal(recs[:, b, :], sums[:, b, :]).then_inc(rec_done, 1)
                    if b + 1 < B:
                        maxima(b + 1)
                    if b:
                        dve.wait_ge(slotT_made, b)
                    dve.wait_ge(rec_done, b + 1)
                    dve.wait_ge(slot_made, (b + 1) * EC)
                    for e in range(EC):
                        dve.tensor_scalar(slot[:, e, :], acc[:, e, :], recs[:, b, e:e + 1], None, ALU.mult)\
                            .then_inc(slot_norm, 1)
                dve.wait_ge(exp_done, 2 * B)
                dve.reciprocal(rect[:, :, :], sumt[:, :, :]).then_inc(sums_done, 1)
                dve.wait_ge(sums_done, 1)
                dve.tensor_scalar(scale[:, :, :], rect[:, :, :], k.gate[:, 3:4], None, ALU.mult).then_inc(sums_done, 1)
                for u in range(EH):
                    dve.wait_ge(out_made, u + 1)
                    dve.tensor_tensor(eo[:, u, :], ob[u % 2][:, 0:D], eb2[:, u, :], ALU.add).then_inc(out_copied, 1)
                dve.wait_ge(sums_done, 2)
                for t in range(NT):
                    b, j = divmod(t, QT)
                    dve.wait_ge(comb_made, t + 1)
                    dve.scalar_tensor_tensor(out=k.x[:, t, :], in0=cb[t % 4][:, 0:D], scalar=scale[:, b, j:j + 1],
                                             in1=k.x[:, t, :], op0=ALU.mult, op1=ALU.add).then_inc(added, 1)

            @block.scalar
            def _(act):
                def take_slots(b):
                    act.wait_ge(slotT_made, b + 1)
                    for c in range(KC):
                        last = act.activation(slotT[:, c, :, :, b, :].rearrange("p u t s -> p t u s"),
                                              tp[:, c, :, :].rearrange("p t (u s) -> p t u s", s=SL), ACT.Copy)
                    last.then_inc(slotT_out, 1)
                for b in range(B):
                    act.wait_ge(mx_done, 2 * b + 1)
                    if b:
                        act.wait_ge(disp_turned, b)
                    for e in range(EC):
                        last = act.activation(eslot[:, e, :], lgs[:, e, :], ACT.Exp, bias=mxs[:, b, e:e + 1],
                                              accum_out=sums[:, b, e:e + 1])
                    last.then_inc(exp_done, 1)
                    act.wait_ge(mx_done, 2 * b + 2)
                    if b >= 2:
                        act.wait_ge(comb_turned, b - 1)
                    for j in range(QT):
                        last = act.activation(etok[:, b % 2, j, :], lgt[:, j, :], ACT.Exp, bias=mxt[:, b, j:j + 1],
                                              accum_out=sumt[:, b, j:j + 1])
                    last.then_inc(exp_done, 1)
                    if b:
                        take_slots(b - 1)
                    act.wait_ge(comb_turned, b + 1)
                    act.activation(comb[:, b, :, :], tr[:, :, :], ACT.Copy).then_inc(comb_out, 1)
                take_slots(B - 1)
                for u in range(EH):
                    act.wait_ge(hid_made, u + 1)
                    for t in range(EC):
                        at = slice(t * HID, t * HID + HID)
                        last = act.activation(hid[at, u, at], hb[u % 2][at, at], ACT.Gelu, bias=eb1[at, u:u + 1])
                    last.then_inc(gelu_done, 1)

            @block.gpsimd
            def _(pool):
                pool.memset(hid[:, :, :], 0.0).then_inc(zeroed, 1)

            @block.sync
            def _(sp):
                with nc.allow_non_contiguous_dma(reason="a bias vector, one number a partition"):
                    for t in range(EC):
                        of_half = slice(t * EH, t * EH + EH)
                        at = slice(t * HID, t * HID + HID)
                        for c in range(KC):
                            sp.dma_start(ew1[:, c, :, t], a["L1_ffn_w1"][of_half, c * P:c * P + P, :]
                                         .rearrange("e p h -> p e h")).then_inc(w_in, 16)
                        sp.dma_start(ew2[at], a["L1_ffn_w2"][of_half].rearrange("e h d -> h e d")).then_inc(w_in, 16)
                        sp.dma_start(eb1[at], a["L1_ffn_b1"][of_half].rearrange("e h -> h e")).then_inc(w_in, 16)
                        sp.dma_start(eb2[at].rearrange("p e d -> p (e d)"),
                                     a["L1_ffn_b2"][of_half].rearrange("(a e) d -> a (e d)", a=1)
                                     .to_broadcast([HID, EH * D])).then_inc(w_in, 16)
                sp.wait_ge(out_copied, EH)
                for c in range(EC):
                    for b in range(B):
                        p0 = (c * B + b) * SL
                        sp.dma_start(k.eo_dram.ap()[b, c * P:c * P + P, :].rearrange("(e s) d -> s e d", s=SL),
                                     eo[p0:p0 + SL, :, :]).then_inc(stored[c], 16)
                for c in range(EC):
                    sp.wait_ge(stored[c], 16 * B)
                    sp.dma_start(so[:, c], k.eo_dram.ap()[:, c * P:c * P + P, :].rearrange("b p d -> p b d"))\
                        .then_inc(back, 16)
                for t in range(0, NT, 2):
                    sp.wait_ge(added, t + 2)
                    b, j = divmod(t, QT)
                    sp.dma_start(out[b, j * P:(j + 2) * P, :].rearrange("(t p) d -> p t d", p=P), k.x[:, t:t + 2, :])\
                        .then_inc(out_stored, 16)
                sp.wait_ge(out_stored, 16 * NT // 2)


def flamingo_kernel(nc, a, out):
    with ExitStack() as ctx:
        k = Core(nc, ctx)
        k.x = k.sb("x", [P, NT, D])
        k.gate = k.sb("gate", [P, 4])
        k.ident = k.sb("ident", [P, P])
        k.identb = k.sb("identb", [P, P], BF16)
        k.anti = k.sb("anti", [P, P], F32R)
        k.ones = k.sb("ones", [P, P])
        k.wt1 = k.sb("wt1", [P, 4, KC, D])
        k.bqk = k.sb("bqk", [P, 2, 2, KC])
        k.bvb = k.sb("bvb", [P, 2, D])
        k.bob = k.sb("bob", [P, D])
        k.b2b = k.sb("b2b", [P, D])
        k.b1c = k.sb("b1c", [P, FT])
        k.phase = k.sb("phase", [P, FT])
        k.coef = k.sb("coef", [P, FT])
        k.scale = k.sb("scale", [P, 1])
        k.ext_dram = nc.dram_tensor("ext_bias", (H, EXT), F32, kind="Internal")
        k.parts = [nc.dram_tensor(f"{w}_parts", (3, D, TOK), BF16, kind="Internal") for w in ("query", "key")]
        k.eo_dram = nc.dram_tensor("expert_out", (B, ES, D), F32, kind="Internal")

        k.ctxT = k.sb("ctxT", [P, KC, TOK])

        k.st = k.sb("st", [P, NT, 6])

        def stacks(scope, layer):
            k.qs = scope.enter_context(nc.sbuf_tensor(f"qs{layer}", [P, STACKS, TOK], BF16))
            k.ks = scope.enter_context(nc.sbuf_tensor(f"ks{layer}", [P, STACKS, TOK], BF16))
            if layer == 0:
                k.slab = scope.enter_context(nc.sbuf_tensor("slab", [P, STACKS, SLAB], F32))

        with nc.sbuf_tensor("v0", [P, NT, H, VW], BF16) as k.v, ExitStack() as scope:
            stacks(scope, 0)
            with nc.sbuf_tensor("hT0", [P, KC, TOK], F32) as k.hT, nc.sbuf_tensor("w0", [P, 3, KC, D], F32) as k.w0:
                with nc.sbuf_tensor("ctxin", [P, NT, D], F32) as k.ctxin:
                    load_phase(k, a)
                turn_phase(k, "t0", k.x, k.hT, stacks=True)
                project_phase(k, 0)
            with nc.sbuf_tensor("oraw0", [P, NT, H, VW], F32) as k.oraw:
                attention_phase(k, 0)
                residual0_phase(k, a)
        with ExitStack() as scope:
            def parts(name, shape):
                return scope.enter_context(nc.sbuf_tensor(name, shape, F32R))
            k.w1p, k.w2p = parts("w1p", [P, 2, KC, F]), parts("w2p", [P, 2, FT, D])
            k.hTp = parts("hTp", [P, 2, KC, TOK])
            with nc.sbuf_tensor("w1", [P, 1, KC, F], F32) as k.w1, nc.sbuf_tensor("w2", [P, 1, FT, D], F32) as k.w2:
                turn_phase(k, "t1", k.x, k.hTp, ffn=a)
            ffn_phase(k)
        k.clear_sems()
        with nc.sbuf_tensor("v1", [P, NT, H, VW], BF16) as k.v, ExitStack() as scope:
            stacks(scope, 1)
            with nc.sbuf_tensor("hT2", [P, KC, TOK], F32) as k.hT:
                turn_phase(k, "t2", k.x, k.hT, stacks=True)
                project_phase(k, 1)
            with nc.sbuf_tensor("oraw1", [P, NT, H, VW], F32) as k.oraw:
                attention_phase(k, 1)
                residual1_phase(k)
        with ExitStack() as scope:
            def sb(name, shape, dt=F32):
                return scope.enter_context(nc.sbuf_tensor(name, shape, dt))
            k.xn = sb("xn", [P, NT, D])
            k.hTp = sb("hT3", [P, 2, KC, TOK], F32R)
            k.mu, k.mup = sb("mu", [P, KC, ES]), sb("mup", [P, 2, KC, ES], F32R)
            k.gamma, k.beta = sb("gamma", [P, D]), sb("beta", [P, D])
            norm_phase(k, a)
            experts_phase(k, a, out)


_OUT = ((B, S, D), "float32")


def kernel(**inputs):
    import numpy as np
    from concourse import bacc
    from concourse.bass_utils import run_bass_kernel_spmd

    nc = bacc.Bacc("TRN2", target_bir_lowering=False, num_devices=1)
    arrays, a = {}, {}
    for name, value in inputs.items():
        array = np.ascontiguousarray(value)
        arrays[f"in_{name}"] = array
        a[name] = nc.dram_tensor(f"in_{name}", array.shape, mybir.dt.from_np(array.dtype), kind="ExternalInput").ap()
    out = nc.dram_tensor("out", _OUT[0], mybir.dt.from_np(np.dtype(_OUT[1])), kind="ExternalOutput").ap()
    flamingo_kernel(nc, a, out)
    result = run_bass_kernel_spmd(nc, [arrays], core_ids=[0])
    return result.results[0]["out"]
```
